# Optimizing a Trainium2 kernel written in Bass

```python
import numpy as np
import jax
import jax.numpy as jnp

def _softmax(x, axis=-1):
    return jax.nn.softmax(x, axis=axis)

def _gelu(x):
    return jax.nn.gelu(x, approximate=True)

def _silu(x):
    return jax.nn.silu(x)

def _sigmoid(x):
    return jax.nn.sigmoid(x)

def _layernorm(x, axis=-1, eps=1e-05):
    m = jnp.mean(x, axis=axis, keepdims=True)
    v = jnp.var(x, axis=axis, keepdims=True)
    return (x - m) / jnp.sqrt(v + eps)

def _scatter_add(tgt, idx, src, axis=0):
    return tgt.at[idx].add(src)

def _segment_sum(src, seg, n):
    return jax.ops.segment_sum(src, seg, n)
kernel_name = 'mk_sandwich_d2_jaxref_r8_921798'

def setup_inputs(seed: int=0):
    np.random.seed(seed)
    _w = jnp.asarray

    def _L0_attn_setup():
        import jax, jax.numpy as jnp
        import numpy as np
        N_HEAD = 16
        LCOMP = 128
        ROPE_THETA = 10000.0

        def _apply_rope(x):
            d = x.shape[-1]
            T = x.shape[-2]
            half = d // 2
            pos = jnp.arange(T, dtype=jnp.float32)
            inv_freq = ROPE_THETA ** (-jnp.arange(half, dtype=jnp.float32) / half)
            ang = pos[:, None] * inv_freq[None, :]
            cos = jnp.repeat(jnp.cos(ang), 2, axis=-1).astype(x.dtype)
            sin = jnp.repeat(jnp.sin(ang), 2, axis=-1).astype(x.dtype)
            x_even = x[..., ::2]
            x_odd = x[..., 1::2]
            rot = jnp.stack((-x_odd, x_even), axis=-1).reshape(x.shape)
            return x * cos + rot * sin
        key = jax.random.key(seed)
        ks = jax.random.split(key, 4)
        B, T, C = (2, 256, 256)
        s = 0.02
        return {'x': jax.random.normal(ks[0], (B, T, C), dtype=jnp.float32), 'W_latent': jax.random.normal(ks[1], (C, LCOMP), dtype=jnp.float32) * s, 'b_latent': jnp.zeros((LCOMP,), dtype=jnp.float32), 'W_d': jax.random.normal(ks[2], (C, N_HEAD * LCOMP), dtype=jnp.float32) * s, 'b_d': jnp.zeros((N_HEAD * LCOMP,), dtype=jnp.float32), 'W_proj': jax.random.normal(ks[3], (N_HEAD * LCOMP, C), dtype=jnp.float32) * s, 'b_proj': jnp.zeros((C,), dtype=jnp.float32)}
    _L0_attn_in = _L0_attn_setup()

    def _L0_ffn_setup():
        import jax, jax.numpy as jnp
        import numpy as np
        TOP_K = 4
        key = jax.random.key(seed)
        ks = jax.random.split(key, 9)
        B, T, D, H, NE = (2, 128, 256, 176, 16)
        s = 0.02
        return {'x': jax.random.normal(ks[0], (B, T, D), jnp.float32), 'gate_w': jax.random.normal(ks[1], (NE, D), jnp.float32) * s, 'gate_b': jax.random.normal(ks[2], (NE,), jnp.float32) * s, 'w1_shared': jax.random.normal(ks[3], (D, H), jnp.float32) * s, 'w2_shared': jax.random.normal(ks[4], (H, D), jnp.float32) * s, 'w3_shared': jax.random.normal(ks[5], (D, H), jnp.float32) * s, 'w1_routed': jax.random.normal(ks[6], (NE, D, H), jnp.float32) * s, 'w2_routed': jax.random.normal(ks[7], (NE, H, D), jnp.float32) * s, 'w3_routed': jax.random.normal(ks[8], (NE, D, H), jnp.float32) * s}
    _L0_ffn_in = _L0_ffn_setup()

    def _L1_attn_setup():
        import jax, jax.numpy as jnp
        import numpy as np
        import math
        HIDDEN = 256
        NUM_HEADS = 16
        HEAD_DIM = HIDDEN // NUM_HEADS
        BATCH = 2
        SEQ = 512
        BLOCK = 128
        TOPK = 64
        NEG = -1000000000.0

        def _split_heads(x):
            n, t, _ = x.shape
            return x.reshape(n, t, NUM_HEADS, HEAD_DIM).transpose(0, 2, 1, 3)

        def _local_attention(q, k, v):
            n, h, t, d = q.shape
            nb = t // BLOCK
            half = BLOCK // 2
            qb = q.reshape(n, h, nb, BLOCK, d)
            win = jnp.arange(nb)[:, None] * BLOCK - half + jnp.arange(2 * BLOCK)[None, :]
            valid = (win >= 0) & (win < t)
            winc = jnp.clip(win, 0, t - 1)
            kb = k[:, :, winc, :]
            vb = v[:, :, winc, :]
            scores = jnp.einsum('nhbqd,nhbkd->nhbqk', qb, kb) / math.sqrt(d)
            scores = jnp.where(valid[None, None, :, None, :], scores, NEG)
            probs = jax.nn.softmax(scores, axis=-1)
            ctx = jnp.einsum('nhbqk,nhbkd->nhbqd', probs, vb)
            return ctx.reshape(n, h, t, d)

        def _global_index(q):
            n, h, t, d = q.shape
            norm = jnp.linalg.norm(q, axis=-1)
            _, top_idx = jax.lax.top_k(norm, TOPK - 2)
            bos = jnp.zeros((n, h, 1), jnp.int32)
            eos = jnp.full((n, h, 1), t - 1, jnp.int32)
            return jnp.concatenate([bos, top_idx.astype(jnp.int32), eos], axis=-1)
        key = jax.random.key(seed)
        ks = jax.random.split(key, 7)
        s = 1.0 / math.sqrt(HIDDEN)
        return {'hidden_states': jax.random.normal(ks[0], (BATCH, SEQ, HIDDEN), jnp.float32), 'Wq': jax.random.normal(ks[1], (HIDDEN, HIDDEN), jnp.float32) * s, 'bq': jnp.zeros((HIDDEN,), jnp.float32), 'Wk': jax.random.normal(ks[2], (HIDDEN, HIDDEN), jnp.float32) * s, 'bk': jnp.zeros((HIDDEN,), jnp.float32), 'Wv': jax.random.normal(ks[3], (HIDDEN, HIDDEN), jnp.float32) * s, 'bv': jnp.zeros((HIDDEN,), jnp.float32)}
    _L1_attn_in = _L1_attn_setup()

    def _L1_ffn_setup():
        import jax, jax.numpy as jnp
        import numpy as np
        DIM = 256
        HID = 704
        ZERO_POINT = 128.0

        def _qlinear(x, wq, scale):
            W = (wq.astype(jnp.float32) - ZERO_POINT) * scale[:, None]
            return jnp.einsum('bsd,hd->bsh', x, W)
        key = jax.random.key(seed)
        ks = jax.random.split(key, 7)
        B, S = (4, 256)
        sg = jax.random.uniform(ks[1], (HID,)) * (0.02 / np.sqrt(DIM)) + 0.0001
        su = jax.random.uniform(ks[3], (HID,)) * (0.02 / np.sqrt(DIM)) + 0.0001
        sd = jax.random.uniform(ks[5], (DIM,)) * (0.02 / np.sqrt(HID)) + 0.0001
        return {'x': jax.random.normal(ks[0], (B, S, DIM), dtype=jnp.float32), 'wq_gate': jax.random.randint(ks[2], (HID, DIM), 0, 32, dtype=jnp.int32), 's_gate': sg, 'wq_up': jax.random.randint(ks[4], (HID, DIM), 0, 32, dtype=jnp.int32), 's_up': su, 'wq_down': jax.random.randint(ks[6], (DIM, HID), 0, 32, dtype=jnp.int32), 's_down': sd}
    _L1_ffn_in = _L1_ffn_setup()
    _d = {'L0_attn_x': _L0_attn_in['x'], 'L0_attn_W_latent': _L0_attn_in['W_latent'], 'L0_attn_b_latent': _L0_attn_in['b_latent'], 'L0_attn_W_d': _L0_attn_in['W_d'], 'L0_attn_b_d': _L0_attn_in['b_d'], 'L0_attn_W_proj': _L0_attn_in['W_proj'], 'L0_attn_b_proj': _L0_attn_in['b_proj'], 'L0_ffn_gate_w': _L0_ffn_in['gate_w'], 'L0_ffn_gate_b': _L0_ffn_in['gate_b'], 'L0_ffn_w1_shared': _L0_ffn_in['w1_shared'], 'L0_ffn_w2_shared': _L0_ffn_in['w2_shared'], 'L0_ffn_w3_shared': _L0_ffn_in['w3_shared'], 'L0_ffn_w1_routed': _L0_ffn_in['w1_routed'], 'L0_ffn_w2_routed': _L0_ffn_in['w2_routed'], 'L0_ffn_w3_routed': _L0_ffn_in['w3_routed'], 'L1_attn_Wq': _L1_attn_in['Wq'], 'L1_attn_bq': _L1_attn_in['bq'], 'L1_attn_Wk': _L1_attn_in['Wk'], 'L1_attn_bk': _L1_attn_in['bk'], 'L1_attn_Wv': _L1_attn_in['Wv'], 'L1_attn_bv': _L1_attn_in['bv'], 'L1_ffn_wq_gate': _L1_ffn_in['wq_gate'], 'L1_ffn_s_gate': _L1_ffn_in['s_gate'], 'L1_ffn_wq_up': _L1_ffn_in['wq_up'], 'L1_ffn_s_up': _L1_ffn_in['s_up'], 'L1_ffn_wq_down': _L1_ffn_in['wq_down'], 'L1_ffn_s_down': _L1_ffn_in['s_down']}
    _x0 = _d['L0_attn_x']
    _d['L0_attn_x'] = jax.random.normal(jax.random.fold_in(jax.random.key(seed), 1), (8, 256, 256), dtype=_x0.dtype)
    del _x0
    return _d

def reference(L0_attn_x, L0_attn_W_latent, L0_attn_b_latent, L0_attn_W_d, L0_attn_b_d, L0_attn_W_proj, L0_attn_b_proj, L0_ffn_gate_w, L0_ffn_gate_b, L0_ffn_w1_shared, L0_ffn_w2_shared, L0_ffn_w3_shared, L0_ffn_w1_routed, L0_ffn_w2_routed, L0_ffn_w3_routed, L1_attn_Wq, L1_attn_bq, L1_attn_Wk, L1_attn_bk, L1_attn_Wv, L1_attn_bv, L1_ffn_wq_gate, L1_ffn_s_gate, L1_ffn_wq_up, L1_ffn_s_up, L1_ffn_wq_down, L1_ffn_s_down):

    def _L0_attn_ref(x, W_latent, b_latent, W_d, b_d, W_proj, b_proj):
        import jax, jax.numpy as jnp
        import numpy as np
        N_HEAD = 16
        LCOMP = 128
        ROPE_THETA = 10000.0

        def _apply_rope(x):
            d = x.shape[-1]
            T = x.shape[-2]
            half = d // 2
            pos = jnp.arange(T, dtype=jnp.float32)
            inv_freq = ROPE_THETA ** (-jnp.arange(half, dtype=jnp.float32) / half)
            ang = pos[:, None] * inv_freq[None, :]
            cos = jnp.repeat(jnp.cos(ang), 2, axis=-1).astype(x.dtype)
            sin = jnp.repeat(jnp.sin(ang), 2, axis=-1).astype(x.dtype)
            x_even = x[..., ::2]
            x_odd = x[..., 1::2]
            rot = jnp.stack((-x_odd, x_even), axis=-1).reshape(x.shape)
            return x * cos + rot * sin
        B, T, C = x.shape
        kv = x @ W_latent + b_latent
        q = (x @ W_d + b_d).reshape(B, T, N_HEAD, LCOMP).transpose(0, 2, 1, 3)
        q_rot = _apply_rope(q)
        k_rot = _apply_rope(kv)
        scale = 1.0 / np.sqrt(LCOMP)
        att = jnp.einsum('bhtd,bsd->bhts', q_rot, k_rot) * scale
        causal = jnp.tril(jnp.ones((T, T), dtype=bool))
        att = jnp.where(causal[None, None], att, -jnp.inf)
        att = jax.nn.softmax(att, axis=-1)
        y = jnp.einsum('bhts,bsd->bhtd', att, kv)
        y = y.transpose(0, 2, 1, 3).reshape(B, T, N_HEAD * LCOMP)
        return y @ W_proj + b_proj

    def _L0_ffn_ref(x, gate_w, gate_b, w1_shared, w2_shared, w3_shared, w1_routed, w2_routed, w3_routed):
        import jax, jax.numpy as jnp
        import numpy as np
        TOP_K = 4
        n_experts = w1_routed.shape[0]
        logits = jnp.einsum('ed,btd->bte', gate_w, x)
        scores = jax.nn.sigmoid(logits) + gate_b
        weights, indices = jax.lax.top_k(scores, TOP_K)
        weights = weights / weights.sum(-1, keepdims=True)
        shared_out = jax.nn.silu(x @ w1_shared) * (x @ w3_shared) @ w2_shared
        one_hot = jax.nn.one_hot(indices, n_experts, dtype=x.dtype)
        router_probs = (weights[..., None] * one_hot).sum(-2)
        h1 = jnp.einsum('btd,edc->btec', x, w1_routed)
        h2 = jnp.einsum('btd,edc->btec', x, w3_routed)
        h3 = jax.nn.silu(h1 * h2)
        experts_out = jnp.einsum('btec,ecd->bted', h3, w2_routed)
        routed_out = jnp.einsum('bted,bte->btd', experts_out, router_probs)
        return shared_out + routed_out

    def _L1_attn_ref(hidden_states, Wq, bq, Wk, bk, Wv, bv):
        import jax, jax.numpy as jnp
        import numpy as np
        import math
        HIDDEN = 256
        NUM_HEADS = 16
        HEAD_DIM = HIDDEN // NUM_HEADS
        BATCH = 2
        SEQ = 512
        BLOCK = 128
        TOPK = 64
        NEG = -1000000000.0

        def _split_heads(x):
            n, t, _ = x.shape
            return x.reshape(n, t, NUM_HEADS, HEAD_DIM).transpose(0, 2, 1, 3)

        def _local_attention(q, k, v):
            n, h, t, d = q.shape
            nb = t // BLOCK
            half = BLOCK // 2
            qb = q.reshape(n, h, nb, BLOCK, d)
            win = jnp.arange(nb)[:, None] * BLOCK - half + jnp.arange(2 * BLOCK)[None, :]
            valid = (win >= 0) & (win < t)
            winc = jnp.clip(win, 0, t - 1)
            kb = k[:, :, winc, :]
            vb = v[:, :, winc, :]
            scores = jnp.einsum('nhbqd,nhbkd->nhbqk', qb, kb) / math.sqrt(d)
            scores = jnp.where(valid[None, None, :, None, :], scores, NEG)
            probs = jax.nn.softmax(scores, axis=-1)
            ctx = jnp.einsum('nhbqk,nhbkd->nhbqd', probs, vb)
            return ctx.reshape(n, h, t, d)

        def _global_index(q):
            n, h, t, d = q.shape
            norm = jnp.linalg.norm(q, axis=-1)
            _, top_idx = jax.lax.top_k(norm, TOPK - 2)
            bos = jnp.zeros((n, h, 1), jnp.int32)
            eos = jnp.full((n, h, 1), t - 1, jnp.int32)
            return jnp.concatenate([bos, top_idx.astype(jnp.int32), eos], axis=-1)
        q = _split_heads(hidden_states @ Wq + bq)
        k = _split_heads(hidden_states @ Wk + bk)
        v = _split_heads(hidden_states @ Wv + bv)
        n, h, t, d = q.shape
        ctx = _local_attention(q, k, v)
        idx = _global_index(q)
        qg = jnp.take_along_axis(q, idx[..., None], axis=-2)
        g_scores = jnp.einsum('nhqd,nhkd->nhqk', qg, k) / math.sqrt(d)
        g_probs = jax.nn.softmax(g_scores, axis=-1)
        g_ctx = jnp.einsum('nhqk,nhkd->nhqd', g_probs, v)
        bn = jnp.arange(n)[:, None, None]
        bh = jnp.arange(h)[None, :, None]
        ctx = ctx.at[bn, bh, idx].set(g_ctx)
        out = ctx.transpose(0, 2, 1, 3).reshape(n, t, h * d)
        return out

    def _L1_ffn_ref(x, wq_gate, s_gate, wq_up, s_up, wq_down, s_down):
        import jax, jax.numpy as jnp
        import numpy as np
        DIM = 256
        HID = 704
        ZERO_POINT = 128.0

        def _qlinear(x, wq, scale):
            W = (wq.astype(jnp.float32) - ZERO_POINT) * scale[:, None]
            return jnp.einsum('bsd,hd->bsh', x, W)
        gate = _qlinear(x, wq_gate, s_gate)
        gate = jax.nn.silu(gate)
        up = _qlinear(x, wq_up, s_up)
        return _qlinear(gate * up, wq_down, s_down)
    x = L0_attn_x
    x = x + _layernorm(_L0_attn_ref(_layernorm(x, axis=-1), L0_attn_W_latent, L0_attn_b_latent, L0_attn_W_d, L0_attn_b_d, L0_attn_W_proj, L0_attn_b_proj), axis=-1)
    x = x + _layernorm(_L0_ffn_ref(_layernorm(x, axis=-1), L0_ffn_gate_w, L0_ffn_gate_b, L0_ffn_w1_shared, L0_ffn_w2_shared, L0_ffn_w3_shared, L0_ffn_w1_routed, L0_ffn_w2_routed, L0_ffn_w3_routed), axis=-1)
    x = x + _layernorm(_L1_attn_ref(_layernorm(x, axis=-1), L1_attn_Wq, L1_attn_bq, L1_attn_Wk, L1_attn_bk, L1_attn_Wv, L1_attn_bv), axis=-1)
    x = x + _layernorm(_L1_ffn_ref(_layernorm(x, axis=-1), L1_ffn_wq_gate, L1_ffn_s_gate, L1_ffn_wq_up, L1_ffn_s_up, L1_ffn_wq_down, L1_ffn_s_down), axis=-1)
    return x

_drawn_inputs = setup_inputs


def setup_inputs(seed=0):
    import zlib

    import numpy as np

    out = dict(_drawn_inputs(seed))
    spreads = {'L0_attn_b_latent': (0.0, 0.1),
     'L0_attn_b_d': (0.0, 0.353),
     'L0_attn_b_proj': (0.0, 0.1),
     'L1_attn_bq': (0.0, 0.8),
     'L1_attn_bk': (0.0, 0.8),
     'L1_attn_bv': (0.0, 0.1)}
    factors = {}
    for name, (base, spread) in spreads.items():
        noise = np.random.default_rng([zlib.crc32(name.encode()), seed]).standard_normal(out[name].shape)
        drawn = base * np.exp(spread * noise) if base else spread * noise
        out[name] = jnp.asarray(drawn.astype(out[name].dtype))
    for name, factor in factors.items():
        out[name] = (out[name] * factor).astype(out[name].dtype)
    return out
```

```python
from contextlib import ExitStack

import concourse.bass as bass
from concourse import mybir

F32 = mybir.dt.float32
F32R = mybir.dt.float32r
BF16 = mybir.dt.bfloat16
I32 = mybir.dt.int32
ALU = mybir.AluOpType
ACT = mybir.ActivationFunctionType
AX = mybir.AxisListType
ds = bass.ds

P = 128
NSEQ, T, D = 8, 256, 256
N = NSEQ * T
NT = N // P
KT = D // P
EPS = 1e-5
HEADS0, LAT = 16, 128
NE, TOPK, HE = 16, 4, 176
NSH = -(-HE // P)
NRT = NE * HE // P
HEADS1, HD = 16, 16
NGLOBAL = 62
HID = 704
HIDT = -(-HID // P)
LOWEST = -3.0e38
NOTE = 1.0e9


def semaphore(nc, ctx, name):
    s = ctx.enter_context(nc.semaphore(name))
    ctx.callback(nc.sync.sem_clear, s)
    return s


class Memory:

    def __init__(self, nc, ctx, io):
        def sb(name, shape, dt=F32):
            return ctx.enter_context(nc.sbuf_tensor(name, shape, dt))

        self.io = io
        self.x = sb("x_res", [P, NT * D])
        self.branch = sb("branch", [P, NT * D])
        self.xt = None
        self.ident = sb("ident", [P, P])
        self.half = sb("minus_half", [P, NT])


def wait(eng, s, value):
    if not isinstance(value, int) or value > 0:
        eng.wait_ge(s, value)


def norm_transpose(nc, m, tag, first=False, last=False, prefetch=None):
    LSHIFT, LADD, LSTAT, LNORM, LSPLIT = (1, 2, 3, 4, 5) if not first else (0, 0, 0, 1, 2)
    MOST = LADD if last else LSPLIT
    LOADS = 4 if first else 0
    BRANCH, X = 0, 1
    with ExitStack() as ctx:
        def sb(name, shape, dt=F32):
            return ctx.enter_context(nc.sbuf_tensor(f"{tag}_{name}", shape, dt))

        def sem(name):
            return semaphore(nc, ctx, f"{tag}_{name}")

        stats = sb("stats", [P, 2, 2, 6])
        mv = sb("mv", [P, 2, NT, 2])
        ve = sb("ve", [P, 2, NT])
        minus_mean = sb("minus_mean", [P, 2, NT])
        rstd = sb("rstd", [P, 2, NT])
        shift = sb("shift", [P, 2, NT])
        normed = sb("normed", [P, 2, 2 * D])
        xn = sb("xn", [P, 2, 2 * D])
        turned = [ctx.enter_context(nc.psum_tensor(f"{tag}_turned{k}", [P, KT, T], F32)) for k in range(2)]
        loaded = [sem(f"loaded{k}") for k in range(LOADS)]
        consts = sem("consts")
        gap = sem("gap")
        moments = [sem("moments_b"), sem("moments_x")]
        rstd_ready = [sem("rstd_b"), sem("rstd_x")]
        shift_ready = [sem("shift_b"), sem("shift_x")]
        normed_ready = sem("normed_ready")
        xn_ready = sem("xn_ready")
        turned_ready = sem("turned_ready")
        high_ready = sem("high_ready")
        low_ready = sem("low_ready")
        x_final = sem("x_final")
        stored = sem("stored")
        block = ctx.enter_context(nc.Block())

        def steps(body):
            for s in range(NSEQ + MOST):
                body(lambda lag: s - lag if 0 <= s - lag < NSEQ else None)

        def pair(b):
            return slice(b * 2 * D, (b + 1) * 2 * D)

        if first:
            @block.sync
            def _(sp):
                sp.dma_start(m.ident[:, :], m.io["ident"]).then_inc(consts, 16)
                for k in range(LOADS):
                    n = NSEQ // LOADS
                    sp.dma_start(m.x[:, k * n * 2 * D:(k + 1) * n * 2 * D].rearrange("p (u d) -> p u d", u=2 * n),
                                 m.io["x"][k * n * T:(k + 1) * n * T, :].rearrange("(u p) d -> p u d", p=P)
                                 ).then_inc(loaded[k], 16)
        if prefetch:
            block.sync(prefetch)
        if last:
            @block.sync
            def _(sp):
                with sp.Fori(0, NSEQ) as b:
                    sp.wait_ge(x_final, b + 1)
                    sp.dma_start(m.io["out"][ds(b * T, T), :].rearrange("(u p) d -> p u d", p=P),
                                 m.x[:, ds(b * 2 * D, 2 * D)].rearrange("p (u d) -> p u d", u=2)
                                 ).then_inc(stored, 16)
                sp.wait_ge(stored, 16 * NSEQ)

        @block.gpsimd
        def _(pool):
            if first:
                pool.memset(m.half[:, :], -0.5).then_inc(x_final, 1)
                pool.wait_ge(x_final, 1)

            def factors(of, b):
                at = slice(2 * b, 2 * b + 2)
                pool.wait_ge(moments[of], b + 1)
                pool.tensor_tensor(rstd[:, of, at], ve[:, of, at], m.half[:, at], ALU.pow).then_inc(rstd_ready[of], 1)
                pool.wait_ge(rstd_ready[of], b + 1)
                pool.tensor_tensor(shift[:, of, at], minus_mean[:, of, at], rstd[:, of, at], ALU.mult).then_inc(shift_ready[of], 1)

            def step(at):
                if not first and (b := at(LADD)) is not None:
                    pool.wait_ge(normed_ready, b + 1)
                    pool.tensor_tensor(m.x[:, pair(b)], m.x[:, pair(b)], normed[:, b % 2, :], ALU.add).then_inc(x_final, 1)
                if not first and (b := at(0)) is not None:
                    factors(BRANCH, b)
                if not last and (b := at(LSTAT)) is not None:
                    factors(X, b)
            steps(step)

        @block.vector
        def _(dve):
            count = 0

            def step(at):
                nonlocal count
                todo = []
                if not last and (b := at(LSTAT)) is not None:
                    if first:
                        dve.wait_ge(loaded[b * LOADS // NSEQ], 16)
                    else:
                        dve.wait_ge(x_final, b + 1)
                    todo.append((X, b, m.x))
                if not first and (b := at(0)) is not None:
                    todo.append((BRANCH, b, m.branch))
                for of, b, src in todo:
                    for u in range(2):
                        dve.bn_stats(stats[:, of, u, :], src[:, (2 * b + u) * D:(2 * b + u + 1) * D]).then_inc(gap, 1)
                        count += 1
                if todo:
                    dve.wait_ge(gap, count)
                for of, b, src in todo:
                    for u in range(2):
                        dve.bn_aggr(mv[:, of, 2 * b + u, :], stats[:, of, u, :]).then_inc(gap, 1)
                        count += 1
                if todo:
                    dve.wait_ge(gap, count)
                for of, b, src in todo:
                    both = slice(2 * b, 2 * b + 2)
                    dve.tensor_scalar(minus_mean[:, of, both], mv[:, of, both, 0], -1.0, None, ALU.mult)
                    dve.tensor_scalar(ve[:, of, both], mv[:, of, both, 1], EPS, None, ALU.add).then_inc(moments[of], 1)
                if not last and (b := at(LSPLIT)) is not None:
                    dve.wait_ge(high_ready, b + 1)
                    tokens = slice(b * T, (b + 1) * T)
                    dve.tensor_tensor(m.xt[:, 1, :, tokens], turned[b % 2][:, :, :], m.xt[:, 0, :, tokens].bitcast(F32),
                                      ALU.subtract).then_inc(low_ready, 1)
            steps(step)

        @block.scalar
        def _(act):
            def norm(of, b, out, src, ready):
                act.wait_ge(shift_ready[of], b + 1)
                for u in range(2):
                    t = 2 * b + u
                    ins = act.activation(out[:, b % 2, u * D:(u + 1) * D], src[:, t * D:(t + 1) * D], ACT.Identity,
                                         scale=rstd[:, of, t:t + 1], bias=shift[:, of, t:t + 1])
                ins.then_inc(ready, 1)

            def step(at):
                if not first and (b := at(LSHIFT)) is not None:
                    wait(act, x_final, b - 1)
                    norm(BRANCH, b, normed, m.branch, normed_ready)
                if not last and (b := at(LSPLIT)) is not None:
                    act.wait_ge(turned_ready, b + 1)
                    act.copy(m.xt[:, 0, :, b * T:(b + 1) * T], turned[b % 2][:, :, :]).then_inc(high_ready, 1)
                if not last and (b := at(LNORM)) is not None:
                    wait(act, turned_ready, b - 1)
                    norm(X, b, xn, m.x, xn_ready)
            steps(step)

        if last:
            return

        @block.tensor
        def _(pe):
            if first:
                pe.wait_ge(consts, 16)

            def step(at):
                if (b := at(LNORM)) is not None:
                    wait(pe, low_ready, b - 1)
                    pe.wait_ge(xn_ready, b + 1)
                    for u in range(2):
                        for k in range(KT):
                            mm = pe.transpose(turned[b % 2][:, k, u * P:(u + 1) * P],
                                              xn[:, b % 2, u * D + k * P:u * D + (k + 1) * P], m.ident[:, :])
                    mm.then_inc(turned_ready, 1)
            steps(step)


def lagged_steps(eng, rounds, width, most, body):
    def one_round(b):
        known = isinstance(b, int)
        for i in range(width if not (known and b == rounds) else most):
            def at(lag, i=i):
                if i >= lag:
                    return None if known and b == rounds else (b, i - lag)
                return None if known and b == 0 else (b - 1, i - lag + width)
            body(at)
    one_round(0)
    with eng.Fori(1, rounds) as b:
        one_round(b)
    one_round(rounds)


def split_matmul(pe, out, stationary, moving, start, stop):
    n = len(stationary)
    for k, ((sh, sl), (mh, ml)) in enumerate(zip(stationary, moving)):
        pe.matmul(out, sh, mh, start=start and k == 0, stop=False, skip_group_check=True)
        pe.matmul(out, sh, ml, start=False, stop=False, skip_group_check=True)
        mm = pe.matmul(out, sl, mh, start=False, stop=stop and k == n - 1, skip_group_check=True)
    return mm


def latent_attention(nc, m):
    with ExitStack() as ctx:
        def sb(name, shape, dt=F32):
            return ctx.enter_context(nc.sbuf_tensor(name, shape, dt))

        wd = sb("wd", [P, 2, KT, HEADS0 * LAT], F32R)
        wp = sb("wp", [P, 2, HEADS0, D], F32R)
        krot = sb("krot", [P, 2, N], F32R)
        v32 = m.branch[:, :].rearrange("p (b n) -> p b n", b=NSEQ)[:, :, 0:2 * LAT]
        trig = sb("trig", [P, 2, T])
        bd = sb("bd", [P, HEADS0])
        mask = sb("mask", [P, 3 * P])
        bproj = sb("bproj", [P, D])
        w = dict(wd=wd, wp=wp, krot=krot, v32=v32, trig=trig, bd=bd, mask=mask, bproj=bproj)
        latent_keys(nc, m, w)
        latent_heads(nc, m, w)


def latent_keys(nc, m, w):
    with ExitStack() as ctx:
        def sb(name, shape, dt=F32):
            return ctx.enter_context(nc.sbuf_tensor(name, shape, dt))

        def sem(name):
            return semaphore(nc, ctx, name)

        CH = 512
        raw = sb("w_raw", [P, 4096])
        wl_raw = sb("wl_raw", [P, KT * LAT])
        wl = sb("wl", [P, 2, KT, LAT], F32R)
        bl = sb("bl", [P, 1])
        kv = sb("kv", [P, 2, CH])
        rot = sb("k_rot", [P, 2, CH])
        part = sb("k_part", [P, CH])
        lat_ps = [ctx.enter_context(nc.psum_tensor(f"lat_ps{k}", [P, CH], F32)) for k in range(2)]
        val_ps = [ctx.enter_context(nc.psum_tensor(f"val_ps{k}", [P, CH], F32)) for k in range(2)]
        small = sem("kv_small")
        wd_in, wp_in = sem("wd_in"), sem("wp_in")
        wl_split, wd_high, wd_done, wp_high = sem("wl_split"), sem("wd_high"), sem("wd_done"), sem("wp_high")
        lat_done, kv_ready, rot_chain, khigh, val_done, val_out = (sem("lat_done"), sem("kv_ready"), sem("rot_chain"),
                                                                   sem("khigh"), sem("val_done"), sem("val_out"))
        split_done = sem("split_done")
        block = ctx.enter_context(nc.Block())

        @block.sync
        def _(sp):
            for dst, name in ((wl_raw[:, :], "wl"), (bl[:, :], "bl"), (w["trig"][:, :, :], "trig"), (w["bd"][:, :], "bd"),
                              (w["mask"][:, :], "mask"), (w["bproj"][:, :], "bproj")):
                sp.dma_start(dst, m.io[name]).then_inc(small, 16)
            sp.dma_start(raw[:, :], m.io["wd"]).then_inc(wd_in, 16)
            sp.wait_ge(wd_done, 1)
            sp.dma_start(raw[:, :], m.io["wp"]).then_inc(wp_in, 16)

        @block.scalar
        def _(act):
            act.wait_ge(small, 96)
            act.copy(wl[:, 0, :, :].rearrange("p k n -> p (k n)"), wl_raw[:, :]).then_inc(wl_split, 1)
            for c in range(4):
                act.wait_ge(lat_done, c + 1)
                if c >= 2:
                    act.wait_ge(val_done, c - 1)
                    act.wait_ge(rot_chain, 5 * (c - 2) + 4)
                act.activation(kv[:, c % 2, :], lat_ps[c % 2][:, :], ACT.Identity, bias=bl[:, 0:1]).then_inc(kv_ready, 1)
                act.wait_ge(rot_chain, 5 * c + 4)
                act.copy(w["krot"][:, 0, c * CH:(c + 1) * CH], rot[:, c % 2, :]).then_inc(khigh, 1)
                act.wait_ge(val_done, c + 1)
                act.copy(w["v32"][:, 2 * c:2 * c + 2, :], val_ps[c % 2][:, :].rearrange("p (b n) -> p b n", b=2)).then_inc(val_out, 1)
            act.wait_ge(wd_in, 16)
            act.copy(w["wd"][:, 0, :, :].rearrange("p k n -> p (k n)"), raw[:, :]).then_inc(wd_high, 1)
            act.wait_ge(wp_in, 16)
            act.copy(w["wp"][:, 0, :, :].rearrange("p k n -> p (k n)"), raw[:, :]).then_inc(wp_high, 1)

        @block.vector
        def _(dve):
            dve.wait_ge(small, 96)
            dve.wait_ge(wl_split, 1)
            dve.tensor_tensor(wl[:, 1, :, :].rearrange("p k n -> p (k n)"), wl_raw[:, :],
                              wl[:, 0, :, :].rearrange("p k n -> p (k n)").bitcast(F32),
                              ALU.subtract).then_inc(wl_split, 1)
            cos = w["trig"][:, 0:1, :].to_broadcast([P, 2, T])
            for c in range(4):
                dve.wait_ge(kv_ready, c + 1)
                if c >= 2:
                    dve.wait_ge(split_done, c - 1)
                src = kv[:, c % 2, :].rearrange("p (b t) -> p b t", b=2)
                dst = rot[:, c % 2, :].rearrange("p (b t) -> p b t", b=2)
                prt = part[:, :].rearrange("p (b t) -> p b t", b=2)
                dve.tensor_tensor(dst, src, cos, ALU.mult).then_inc(rot_chain, 1)
                for a, z in ((0, 64), (64, 0)):
                    if c:
                        dve.wait_ge(rot_chain, 5 * c - 1)
                    dve.tensor_tensor(prt[a:a + 64], src[z:z + 64], w["trig"][z:z + 64, 1:2, :].to_broadcast([64, 2, T]),
                                      ALU.mult).then_inc(rot_chain, 1)
                dve.wait_ge(rot_chain, 5 * c + 3)
                dve.tensor_tensor(rot[:, c % 2, :], rot[:, c % 2, :], part[:, :], ALU.add).then_inc(rot_chain, 1)
                dve.wait_ge(khigh, c + 1)
                dve.wait_ge(rot_chain, 5 * c + 4)
                dve.tensor_tensor(w["krot"][:, 1, c * CH:(c + 1) * CH], rot[:, c % 2, :],
                                  w["krot"][:, 0, c * CH:(c + 1) * CH].bitcast(F32), ALU.subtract).then_inc(split_done, 1)
                dve.wait_ge(split_done, c + 1)
                dve.sem_inc(rot_chain, 1)
            for name, high, done in (("wd", wd_high, wd_done), ("wp", wp_high, None)):
                dve.wait_ge(high, 1)
                ins = dve.tensor_tensor(w[name][:, 1, :, :].rearrange("p k n -> p (k n)"), raw[:, :],
                                        w[name][:, 0, :, :].rearrange("p k n -> p (k n)").bitcast(F32), ALU.subtract)
                if done is not None:
                    ins.then_inc(done, 1)

        @block.tensor
        def _(pe):
            pe.wait_ge(wl_split, 2)

            def turn(c):
                pe.wait_ge(kv_ready, c + 1)
                if c >= 2:
                    pe.wait_ge(val_out, c - 1)
                for s in range(4):
                    mm = pe.transpose(val_ps[c % 2][:, s * P:(s + 1) * P], kv[:, c % 2, s * P:(s + 1) * P], m.ident[:, :])
                mm.then_inc(val_done, 1)

            for c in range(4):
                if c >= 2:
                    pe.wait_ge(kv_ready, c - 1)
                at = slice(c * CH, (c + 1) * CH)
                split_matmul(pe, lat_ps[c % 2][:, :], [(wl[:, 0, k, :], wl[:, 1, k, :]) for k in range(KT)],
                             [(m.xt[:, 0, k, at], m.xt[:, 1, k, at]) for k in range(KT)], True, True).then_inc(lat_done, 1)
                if c >= 1:
                    turn(c - 1)
            turn(3)


def latent_heads(nc, m, w):
    PAIRS = HEADS0 // 2
    SCALE = LAT ** -0.5
    LQ, LROT, LSUM, LS, LNORM, LT, LV, LO, LOUT = 0, 1, 2, 3, 4, 5, 6, 7, 8
    with ExitStack() as ctx:
        def sb(name, shape, dt=F32):
            return ctx.enter_context(nc.sbuf_tensor(name, shape, dt))

        def sem(name):
            return semaphore(nc, ctx, name)

        def bank(name):
            return ctx.enter_context(nc.psum_tensor(name, [P, 512], F32))

        qb = sb("qb", [P, 2, 2 * T])
        qsum = sb("qsum", [P, 2, 2 * T])
        qpart = sb("qpart", [P, 2 * T])
        qr = sb("qr", [P, 2, 2, 2 * T], F32R)
        probs = sb("probs0", [P, 4, 2, 3 * P])
        top = sb("top0", [P, 4, 4])
        neg = sb("neg0", [P, 4, 4])
        total = sb("total0", [P, 4, 4])
        inv = sb("inv0", [P, 4, 4])
        pt = sb("pt0", [P, 2, 2, 2, 3 * P], F32R)
        v = sb("v0", [P, 2, 2 * LAT], F32R)
        y = sb("y0", [P, 2, 2, 2 * T], F32R)
        q_ps, y_ps, o_ps = bank("q_ps"), bank("y_ps"), bank("o_ps")
        s_ps = [bank("s_ps0"), bank("s_ps1")]
        t_ps = [bank("t_ps0"), bank("t_ps1")]

        q_done, s_done, t_done, y_done, o_done = sem("q_done"), sem("s_done"), sem("t_done"), sem("y_done"), sem("o_done")
        qb_ready, qcos_ready, qpart_ready, qsum_ready, qhigh, qlow = (
            sem("qb_ready"), sem("qcos_ready"), sem("qpart_ready"), sem("qsum_ready"), sem("qhigh"), sem("qlow"))
        masked, neg_ready, exp_ready, inv_ready, probs_ready = (
            sem("masked"), sem("neg_ready"), sem("exp_ready"), sem("inv_ready"), sem("probs_ready"))
        phigh, plow, vhigh, vlow, yhigh, ylow, o_out = (
            sem("phigh"), sem("plow"), sem("vhigh"), sem("vlow"), sem("yhigh"), sem("ylow"), sem("o_out"))
        pause = sem("pause0")
        block = ctx.enter_context(nc.Block())

        def steps(eng, body):
            lagged_steps(eng, NSEQ, PAIRS, LOUT, body)

        @block.tensor
        def _(pe):
            def step(at):
                if s := at(LT):
                    b, j = s
                    g = b * PAIRS + j
                    r = j % 2
                    for u in range(2):
                        wait(pe, plow, g * 2 + u - 1)
                        pe.wait_ge(probs_ready, g * 2 + u + 1)
                        for k in range(3):
                            mm = pe.transpose(t_ps[u][:, k * P:(k + 1) * P], probs[:, j % 4, u, k * P:(k + 1) * P], m.ident[:, :])
                        mm.then_inc(t_done, 1)
                if s := at(LV):
                    b, j = s
                    g = b * PAIRS + j
                    r = j % 2
                    wait(pe, ylow, g)
                    if j == 0:
                        wait(pe, vlow, b + 1)
                    for u in range(2):
                        wait(pe, plow, g * 2 + u + 1)
                        o = y_ps[:, u * T:(u + 1) * T]
                        split_matmul(pe, o, [(v[:, 0, 0:LAT], v[:, 1, 0:LAT])],
                                     [(pt[:, r, 0, u, 0:2 * P], pt[:, r, 1, u, 0:2 * P])], True, False)
                        mm = split_matmul(pe, y_ps[:, u * T + P:(u + 1) * T], [(v[:, 0, LAT:2 * LAT], v[:, 1, LAT:2 * LAT])],
                                          [(pt[:, r, 0, u, 2 * P:3 * P], pt[:, r, 1, u, 2 * P:3 * P])], False, True)
                    mm.then_inc(y_done, 1)
                if s := at(LS):
                    b, j = s
                    g = b * PAIRS + j
                    r = j % 2
                    wait(pe, qlow, g + 1)
                    for u in range(2):
                        wait(pe, masked, g * 2 + u - 1)
                        for t, cols, keys in ((0, slice(0, P), P), (1, slice(P, 3 * P), 2 * P)):
                            q = [(qr[:, r, 0, u * T + t * P:u * T + t * P + P], qr[:, r, 1, u * T + t * P:u * T + t * P + P])]
                            kk = [(w["krot"][:, 0, ds(b * T, keys)], w["krot"][:, 1, ds(b * T, keys)])]
                            mm = split_matmul(pe, s_ps[u][:, cols], q, kk, True, True)
                        mm.then_inc(s_done, 1)
                if s := at(LQ):
                    b, j = s
                    g = b * PAIRS + j
                    wait(pe, qb_ready, g)
                    for u in range(2):
                        h = 2 * j + u
                        ws = [(w["wd"][:, 0, k, h * LAT:(h + 1) * LAT], w["wd"][:, 1, k, h * LAT:(h + 1) * LAT])
                              for k in range(KT)]
                        xs = [(m.xt[:, 0, k, ds(b * T, T)], m.xt[:, 1, k, ds(b * T, T)]) for k in range(KT)]
                        mm = split_matmul(pe, q_ps[:, u * T:(u + 1) * T], ws, xs, True, True)
                    mm.then_inc(q_done, 1)
                if s := at(LO):
                    b, j = s
                    g = b * PAIRS + j
                    r = j % 2
                    pe.wait_ge(ylow, g + 1)
                    if j == 0:
                        wait(pe, o_out, b)
                    for u in range(2):
                        for t in range(2):
                            ys = [(y[:, r, 0, u * T + t * P:u * T + t * P + P], y[:, r, 1, u * T + t * P:u * T + t * P + P])]
                            ws = [(w["wp"][:, 0, 2 * j + u, :], w["wp"][:, 1, 2 * j + u, :])]
                            mm = split_matmul(pe, o_ps[:, t * D:(t + 1) * D], ys, ws, j == 0 and u == 0 and t == 0,
                                              j == PAIRS - 1 and u == 1)
                    mm.then_inc(o_done, 1)
            steps(pe, step)

        @block.scalar
        def _(act):
            def step(at):
                if s := at(LSUM):
                    b, j = s
                    g = b * PAIRS + j
                    r = j % 2
                    act.wait_ge(qsum_ready, g + 1)
                    wait(act, s_done, g * 2 - 2)
                    act.copy(qr[:, r, 0, :], qsum[:, r, :]).then_inc(qhigh, 1)
                if s := at(LT):
                    b, j = s
                    g = b * PAIRS + j
                    r = j % 2
                    wait(act, y_done, g - 1)
                    for u in range(2):
                        act.wait_ge(t_done, g * 2 + u + 1)
                        act.copy(pt[:, r, 0, u, :], t_ps[u][:, 0:3 * P]).then_inc(phigh, 1)
                if s := at(LV):
                    b, j = s
                    g = b * PAIRS + j
                    r = j % 2
                    act.wait_ge(y_done, g + 1)
                    wait(act, o_done, g - 1)
                    act.copy(y[:, r, 0, :], y_ps[:, :]).then_inc(yhigh, 1)
                if s := at(LV - 1):
                    b, j = s
                    if j == 0:
                        wait(act, y_done, b * PAIRS)
                        act.sem_inc(pause, 1)
                        act.copy(v[:, 0, :], m.branch[:, ds(b * 2 * D, 2 * LAT)]).then_inc(vhigh, 1)
                if s := at(LROT):
                    b, j = s
                    g = b * PAIRS + j
                    r = j % 2
                    act.wait_ge(q_done, g + 1)
                    wait(act, qsum_ready, g - 1)
                    for u in range(2):
                        ins = act.activation(qb[:, r, u * T:(u + 1) * T], q_ps[:, u * T:(u + 1) * T], ACT.Identity,
                                             bias=w["bd"][:, 2 * j + u:2 * j + u + 1])
                    ins.then_inc(qb_ready, 1)
                if s := at(LS):
                    b, j = s
                    g = b * PAIRS + j
                    r = j % 2
                    act.wait_ge(neg_ready, g + 1)
                    for u in range(2):
                        for t, cols in ((0, slice(0, P)), (1, slice(P, 3 * P))):
                            ins = act.activation(probs[:, j % 4, u, cols], probs[:, j % 4, u, cols], ACT.Exp,
                                                 bias=neg[:, j % 4, 2 * u + t:2 * u + t + 1], scale=SCALE,
                                                 accum_out=total[:, j % 4, 2 * u + t:2 * u + t + 1])
                    ins.then_inc(exp_ready, 1)
            steps(act, step)

        @block.gpsimd
        def _(pool):
            cos = w["trig"][:, 0:1, :].to_broadcast([P, 2, T])

            def step(at):
                if s := at(LSUM):
                    b, j = s
                    g = b * PAIRS + j
                    r = j % 2
                    pool.wait_ge(qhigh, g + 1)
                    pool.tensor_tensor(qr[:, r, 1, :], qsum[:, r, :], qr[:, r, 0, :].bitcast(F32), ALU.subtract).then_inc(qlow, 1)
                if s := at(LROT):
                    b, j = s
                    g = b * PAIRS + j
                    r = j % 2
                    wait(pool, qlow, g - 1)
                    pool.wait_ge(qb_ready, g + 1)
                    pool.tensor_tensor(qsum[:, r, :].rearrange("p (u t) -> p u t", u=2),
                                       qb[:, r, :].rearrange("p (u t) -> p u t", u=2), cos, ALU.mult).then_inc(qcos_ready, 1)
            steps(pool, step)

        @block.vector
        def _(dve):
            def step(at):
                if s := at(LSUM):
                    b, j = s
                    g = b * PAIRS + j
                    r = j % 2
                    dve.wait_ge(qcos_ready, g + 1)
                    dve.wait_ge(qpart_ready, g + 1)
                    dve.tensor_tensor(qsum[:, r, :], qsum[:, r, :], qpart[:, :], ALU.add).then_inc(qsum_ready, 1)
                if s := at(LNORM):
                    b, j = s
                    g = b * PAIRS + j
                    r = j % 2
                    dve.wait_ge(exp_ready, g + 1)
                    dve.reciprocal(inv[:, j % 4, :], total[:, j % 4, :]).then_inc(inv_ready, 1)
                    dve.wait_ge(inv_ready, g + 1)
                    for u in range(2):
                        for t, cols in ((0, slice(0, P)), (1, slice(P, 3 * P))):
                            ins = dve.tensor_scalar(probs[:, j % 4, u, cols], probs[:, j % 4, u, cols],
                                                    inv[:, j % 4, 2 * u + t:2 * u + t + 1], None, ALU.mult)
                        ins.then_inc(probs_ready, 1)
                if s := at(LT):
                    b, j = s
                    g = b * PAIRS + j
                    r = j % 2
                    for u in range(2):
                        dve.wait_ge(phigh, g * 2 + u + 1)
                        dve.tensor_tensor(pt[:, r, 1, u, :], t_ps[u][:, 0:3 * P], pt[:, r, 0, u, :].bitcast(F32),
                                          ALU.subtract).then_inc(plow, 1)
                if s := at(LV):
                    b, j = s
                    g = b * PAIRS + j
                    r = j % 2
                    dve.wait_ge(yhigh, g + 1)
                    dve.tensor_tensor(y[:, r, 1, :], y_ps[:, :], y[:, r, 0, :].bitcast(F32), ALU.subtract).then_inc(ylow, 1)
                if s := at(LV - 1):
                    b, j = s
                    if j == 0:
                        dve.wait_ge(vhigh, b + 1)
                        dve.tensor_tensor(v[:, 1, :], m.branch[:, ds(b * 2 * D, 2 * LAT)], v[:, 0, :].bitcast(F32),
                                          ALU.subtract).then_inc(vlow, 1)
                if s := at(LS):
                    b, j = s
                    g = b * PAIRS + j
                    r = j % 2
                    wait(dve, t_done, g * 2 - 6)
                    for u in range(2):
                        dve.wait_ge(s_done, g * 2 + u + 1)
                        dve.sem_inc(pause, 1)
                        for t, cols in ((0, slice(0, P)), (1, slice(P, 3 * P))):
                            ins = dve.tensor_tensor_reduce(probs[:, j % 4, u, cols], s_ps[u][:, cols], w["mask"][:, cols],
                                                           1.0, LOWEST, ALU.add, ALU.max, top[:, j % 4, 2 * u + t:2 * u + t + 1])
                        ins.then_inc(masked, 1)
                    dve.wait_ge(masked, g * 2 + 2)
                    dve.tensor_scalar(neg[:, j % 4, :], top[:, j % 4, :], -SCALE, None, ALU.mult).then_inc(neg_ready, 1)
                if s := at(LROT):
                    b, j = s
                    g = b * PAIRS + j
                    r = j % 2
                    dve.wait_ge(qb_ready, g + 1)
                    wait(dve, qsum_ready, g)
                    for a, z in ((0, 64), (64, 0)):
                        ins = dve.tensor_tensor(qpart[a:a + 64, :].rearrange("p (u t) -> p u t", u=2),
                                                qb[z:z + 64, r, :].rearrange("p (u t) -> p u t", u=2),
                                                w["trig"][z:z + 64, 1:2, :].to_broadcast([64, 2, T]), ALU.mult)
                    ins.then_inc(qpart_ready, 1)
                if s := at(LOUT):
                    b, j = s
                    if j == PAIRS - 1:
                        dve.wait_ge(o_done, (b + 1) * PAIRS)
                        dve.tensor_tensor(m.branch[:, ds(b * 2 * D, 2 * D)].rearrange("p (u d) -> p u d", u=2),
                                          o_ps[:, :].rearrange("p (u d) -> p u d", u=2),
                                          w["bproj"][:, :].rearrange("p (u d) -> p u d", u=1).to_broadcast([P, 2, D]),
                                          ALU.add).then_inc(o_out, 1)
            steps(dve, step)



HT = NSH + NRT
UPC = 2 * KT * P
TILE = UPC + D
CH = 512
NCH = N // CH


def load_tiles(sp, m, e, weights_in, a, z):
    for k in range(a, z):
        sp.dma_start(e["raw"][:, 2 * k * TILE:2 * (k + 1) * TILE], m.io["experts"][:, 2 * k * TILE:2 * (k + 1) * TILE]
                     ).then_inc(weights_in, 16)
        sp.wait_ge(weights_in, 16 * (k + 1))


def router(nc, m, e):
    with ExitStack() as ctx:
        def sb(name, shape, dt=F32):
            return ctx.enter_context(nc.sbuf_tensor(name, shape, dt))

        def sem(name):
            return semaphore(nc, ctx, name)

        WID = NE + TOPK
        sel32 = sb("sel32", [96, NRT * P])
        g_raw = sb("g_raw", [P, KT * P])
        gate = sb("gate", [P, 2, KT, P], F32R)
        gb = sb("gb", [P, 1])
        sig = sb("sig", [NE, 2, CH])
        score = sb("score", [P, NT, WID])
        best = sb("best", [P, NT, 8])
        found = sb("found", [P, NT, WID])
        prob = sb("prob", [P, NT, NE])
        total = sb("rtotal", [P, NT])
        parts = sb("pparts", [P, NT, 96], BF16)
        ident_b = sb("ident_b", [P, P], BF16)
        log_ps = [ctx.enter_context(nc.psum_tensor(f"log_ps{k}", [P, CH], F32)) for k in range(2)]
        score_ps = ctx.enter_context(nc.psum_tensor("score_ps", [P, NT, NE], F32))
        pt_ps = [ctx.enter_context(nc.psum_tensor(f"pt_ps{k}", [P, CH], BF16)) for k in range(2)]
        small, gate_ready, log_done, exp_ready, sig_ready, score_done = (
            sem("r_small"), sem("gate_ready"), sem("log_done"), sem("rexp_ready"), sem("sig_ready"), sem("score_done"))
        chain, parts_ready, turned, out = sem("rchain"), sem("parts_ready"), sem("rturned"), sem("rout")
        block = ctx.enter_context(nc.Block())

        @block.sync
        def _(sp):
            sp.dma_start(g_raw[:, :], m.io["gate"]).then_inc(small, 16)
            sp.dma_start(gb[:, :], m.io["gb"]).then_inc(small, 16)
            sp.dma_start(sel32[:, :], m.io["sel"]).then_inc(small, 16)
            sp.wait_ge(small, 48)

        @block.scalar
        def _(act):
            act.wait_ge(small, 48)
            act.copy(gate[:, 0, :, :].rearrange("p k n -> p (k n)"), g_raw[:, :]).then_inc(gate_ready, 1)
            act.copy(ident_b[:, :], m.ident[:, :]).then_inc(gate_ready, 1)
            act.copy(e["sel"][:, :], sel32[:, :])
            for c in range(NCH):
                act.wait_ge(log_done, c + 1)
                if c >= 2:
                    act.wait_ge(score_done, c - 1)
                act.activation(sig[:, c % 2, :], log_ps[c % 2][0:NE, :], ACT.Exp, scale=-1.0).then_inc(exp_ready, 1)

        @block.vector
        def _(dve):
            dve.memset(parts[:, :, :], 0.0).then_inc(parts_ready, 1)
            dve.memset(score[:, :, NE:WID], LOWEST).then_inc(parts_ready, 1)
            dve.wait_ge(gate_ready, 1)
            dve.tensor_tensor(gate[:, 1, :, :].rearrange("p k n -> p (k n)"), g_raw[:, :],
                              gate[:, 0, :, :].rearrange("p k n -> p (k n)").bitcast(F32), ALU.subtract).then_inc(gate_ready, 1)
            for c in range(NCH):
                s = sig[:, c % 2, :]
                dve.wait_ge(exp_ready, c + 1)
                dve.tensor_scalar(s, s, 1.0, None, ALU.add).then_inc(sig_ready, 1)
                dve.wait_ge(sig_ready, 3 * c + 1)
                dve.reciprocal(s, s).then_inc(sig_ready, 1)
                dve.wait_ge(sig_ready, 3 * c + 2)
                dve.tensor_scalar(s, s, gb[0:NE, 0:1], None, ALU.add).then_inc(sig_ready, 1)
            dve.wait_ge(score_done, NCH)
            dve.tensor_copy(score[:, :, 0:NE], score_ps[:, :, :]).then_inc(chain, 1)
            dve.wait_ge(chain, 1)
            for t in range(NT):
                dve.max(best[:, t, :], score[:, t, 0:NE]).then_inc(chain, 1)
            dve.wait_ge(chain, 1 + NT)
            dve.memset(best[:, :, TOPK:8], LOWEST).then_inc(chain, 1)
            dve.wait_ge(chain, 2 + NT)
            for t in range(NT):
                dve.match_replace(found[:, t, :], best[:, t, :], score[:, t, :], 3.0e38).then_inc(chain, 1)
            dve.wait_ge(chain, 2 + 2 * NT)
            n = 2 + 2 * NT
            dve.tensor_tensor(prob[:, :, :], found[:, :, 0:NE], score[:, :, 0:NE], ALU.not_equal).then_inc(chain, 1)
            dve.wait_ge(chain, n + 1)
            dve.tensor_tensor(prob[:, :, :], prob[:, :, :], score[:, :, 0:NE], ALU.mult).then_inc(chain, 1)
            dve.wait_ge(chain, n + 2)
            dve.tensor_reduce(total[:, :], prob[:, :, :], AX.X, ALU.add).then_inc(chain, 1)
            dve.wait_ge(chain, n + 3)
            dve.reciprocal(total[:, :], total[:, :]).then_inc(chain, 1)
            dve.wait_ge(chain, n + 4)
            dve.tensor_tensor(prob[:, :, :], prob[:, :, :],
                              total[:, :].rearrange("p (t o) -> p t o", o=1).to_broadcast([P, NT, NE]), ALU.mult).then_inc(chain, 1)
            n += 5
            for k in range(3):
                dve.wait_ge(chain, n)
                dve.tensor_copy(parts[:, :, 32 * k:32 * k + NE], prob[:, :, :]).then_inc(chain, 1)
                if k < 2:
                    dve.wait_ge(chain, n + 1)
                    dve.tensor_tensor(prob[:, :, :], prob[:, :, :], parts[:, :, 32 * k:32 * k + NE], ALU.subtract).then_inc(chain, 1)
                n += 2
            dve.wait_ge(chain, n - 1)
            dve.sem_inc(parts_ready, 1)
            for c in range(NCH):
                dve.wait_ge(turned, c + 1)
                dve.tensor_copy(e["pt"][:, c * CH:(c + 1) * CH], pt_ps[c % 2][0:96, :]).then_inc(out, 1)

        @block.tensor
        def _(pe):
            pe.wait_ge(gate_ready, 3)

            def turn(c):
                pe.wait_ge(sig_ready, 3 * c + 3)
                for s in range(4):
                    mm = pe.transpose(score_ps[:, 4 * c + s, :], sig[:, c % 2, s * P:(s + 1) * P], m.ident[0:NE, 0:NE])
                mm.then_inc(score_done, 1)

            for c in range(NCH):
                if c >= 2:
                    pe.wait_ge(exp_ready, c - 1)
                at = slice(c * CH, (c + 1) * CH)
                split_matmul(pe, log_ps[c % 2][:, :], [(gate[:, 0, k, :], gate[:, 1, k, :]) for k in range(KT)],
                             [(m.xt[:, 0, k, at], m.xt[:, 1, k, at]) for k in range(KT)], True, True).then_inc(log_done, 1)
                if c >= 1:
                    turn(c - 1)
            turn(NCH - 1)
            pe.wait_ge(parts_ready, 3)
            for c in range(NCH):
                if c >= 2:
                    pe.wait_ge(out, c - 1)
                for s in range(4):
                    mm = pe.transpose(pt_ps[c % 2][0:96, s * P:(s + 1) * P], parts[:, 4 * c + s, :], ident_b[:, :])
                mm.then_inc(turned, 1)


def experts(nc, m, e, weights_in):
    HEAD = 4
    LSPLIT, LUP, LHID, LDOWN = 0, 1, 2, 3
    with ExitStack() as ctx:
        def sb(name, shape, dt=F32):
            return ctx.enter_context(nc.sbuf_tensor(name, shape, dt))

        def sem(name):
            return semaphore(nc, ctx, name)

        def bank(name):
            return ctx.enter_context(nc.psum_tensor(name, [P, CH], F32))

        raw = e["raw"]
        up = sb("up_w", [P, 2, 2, UPC], F32R)
        down = sb("down_w", [P, 2, 2, D], F32R)
        gated = sb("gated", [P, 2, CH])
        hid = sb("hid", [P, 2, CH])
        h = sb("h_parts", [P, 2, 2, CH], F32R)
        h1_ps = [bank("h1_ps0"), bank("h1_ps1")]
        h3_ps = [bank("h3_ps0"), bank("h3_ps1")]
        w_ps = bank("weight_ps")
        o_ps = [bank("eo_ps0"), bank("eo_ps1")]
        up_high, up_low, down_high, down_low = sem("up_high"), sem("up_low"), sem("down_high"), sem("down_low")
        up_done, weight_done, down_done = sem("up_done"), sem("weight_done"), sem("down_done")
        lifted, product_ready, silu_ready, hid_ready, h_high, h_low = (
            sem("lifted"), sem("product_ready"), sem("silu_ready"), sem("hid_ready"), sem("h_high"), sem("h_low"))
        out_a, out_b, pause = sem("eout_a"), sem("eout_b"), sem("epause")
        block = ctx.enter_context(nc.Block())

        def steps(eng, body):
            def chunk(c):
                known = isinstance(c, int)
                for k in range(HEAD if not (known and c == NCH) else LDOWN + 1):
                    def at(lag, k=k):
                        if k >= lag:
                            return None if known and c == NCH else (c, k - lag, (k - lag) % 2)
                        return None if known and c == 0 else (c - 1, k - lag + HT, (k - lag) % 2)
                    body(at)
                if known and c == NCH:
                    return
                with eng.Fori(0, (HT - HEAD) // 2) as it:
                    for o in range(2):
                        body(lambda lag, o=o: (c, it * 2 + (HEAD + o - lag), (HEAD + o - lag) % 2))
            chunk(0)
            with eng.Fori(1, NCH) as c:
                chunk(c)
            chunk(NCH)

        def shared(k):
            return isinstance(k, int) and k < NSH

        @block.sync
        def _(sp):
            load_tiles(sp, m, e, weights_in, 6, HT // 2)

        @block.scalar
        def _(act):
            def step(at):
                if s := at(LSPLIT):
                    c, k, r = s
                    act.wait_ge(weights_in, (k // 2) * 16 + 16 if isinstance(k, int) else k * 8 + (16 if r == 0 else 8))
                    wait(act, up_done, c * HT + k - 1)
                    act.sem_inc(pause, 1)
                    act.copy(up[:, r, 0, :], raw[:, ds(k * TILE, UPC)]).then_inc(up_high, 1)
                if s := at(LHID):
                    c, k, r = s
                    g = c * HT + k
                    if not shared(k):
                        act.wait_ge(product_ready, c * NRT + k - NSH + 1)
                        act.activation(gated[:, r, :], gated[:, r, :], ACT.Silu).then_inc(silu_ready, 1)
                    wait(act, down_done, g - 1)
                    act.sem_inc(pause, 1)
                    act.copy(down[:, r, 0, :], raw[:, ds(k * TILE + UPC, D)]).then_inc(down_high, 1)
                    act.wait_ge(hid_ready, g + 1)
                    act.copy(h[:, r, 0, :], hid[:, r, :]).then_inc(h_high, 1)
                if s := at(LUP):
                    c, k, r = s
                    g = c * HT + k
                    act.wait_ge(up_done, g + 1)
                    wait(act, hid_ready, g - 1)
                    if shared(k):
                        act.activation(gated[:, r, :], h1_ps[r][:, :], ACT.Silu).then_inc(lifted, 1)
                    else:
                        act.copy(gated[:, r, :], h3_ps[r][:, :]).then_inc(lifted, 1)
                if s := at(LDOWN):
                    c, k, r = s
                    if isinstance(k, int) and k == HT - 1:
                        act.wait_ge(down_done, (c + 1) * HT)
                        act.sem_inc(pause, 1)
                        act.copy(m.branch[:, ds(c * 4 * D, 2 * D)], o_ps[0][:, :]).then_inc(out_a, 1)
            steps(act, step)

        @block.vector
        def _(dve):
            def step(at):
                if s := at(LSPLIT):
                    c, k, r = s
                    g = c * HT + k
                    dve.wait_ge(up_high, g + 1)
                    dve.tensor_tensor(up[:, r, 1, :], raw[:, ds(k * TILE, UPC)], up[:, r, 0, :].bitcast(F32),
                                      ALU.subtract).then_inc(up_low, 1)
                if s := at(LHID):
                    c, k, r = s
                    g = c * HT + k
                    wait(dve, h_low, g - 1)
                    if shared(k):
                        dve.wait_ge(lifted, g + 1)
                        dve.tensor_tensor(hid[:, r, :], gated[:, r, :], h3_ps[r][:, :], ALU.mult).then_inc(hid_ready, 1)
                    else:
                        dve.wait_ge(silu_ready, c * NRT + k - NSH + 1)
                        dve.wait_ge(weight_done, c * NRT + k - NSH + 1)
                        dve.tensor_tensor(hid[:, r, :], gated[:, r, :], w_ps[:, :], ALU.mult).then_inc(hid_ready, 1)
                    dve.wait_ge(down_high, g + 1)
                    dve.tensor_tensor(down[:, r, 1, :], raw[:, ds(k * TILE + UPC, D)], down[:, r, 0, :].bitcast(F32),
                                      ALU.subtract).then_inc(down_low, 1)
                    dve.wait_ge(h_high, g + 1)
                    dve.tensor_tensor(h[:, r, 1, :], hid[:, r, :], h[:, r, 0, :].bitcast(F32), ALU.subtract).then_inc(h_low, 1)
                if s := at(LUP):
                    c, k, r = s
                    if not shared(k):
                        dve.wait_ge(lifted, c * HT + k + 1)
                        dve.tensor_tensor(gated[:, r, :], gated[:, r, :], h1_ps[r][:, :], ALU.mult).then_inc(product_ready, 1)
                if s := at(LDOWN):
                    c, k, r = s
                    if isinstance(k, int) and k == HT - 1:
                        dve.wait_ge(down_done, (c + 1) * HT)
                        dve.tensor_copy(m.branch[:, ds(c * 4 * D + 2 * D, 2 * D)], o_ps[1][:, :]).then_inc(out_b, 1)
            steps(dve, step)

        @block.tensor
        def _(pe):
            def step(at):
                if s := at(LHID):
                    c, k, r = s
                    g = c * HT + k
                    if not shared(k):
                        wait(pe, hid_ready, g)
                        pe.matmul(w_ps[:, :], e["sel"][:, ds((k - NSH) * P, P)], e["pt"][:, ds(c * CH, CH)],
                                  start=True, stop=True).then_inc(weight_done, 1)
                if s := at(LUP):
                    c, k, r = s
                    g = c * HT + k
                    pe.wait_ge(up_low, g + 1)
                    wait(pe, hid_ready, g - 1)
                    xs = [(m.xt[:, 0, kt, ds(c * CH, CH)], m.xt[:, 1, kt, ds(c * CH, CH)]) for kt in range(KT)]
                    for j, o in ((1, h3_ps[r]), (0, h1_ps[r])):
                        ws = [tuple(up[:, r, q, (j * KT + kt) * P:(j * KT + kt + 1) * P] for q in range(2)) for kt in range(KT)]
                        mm = split_matmul(pe, o[:, :], ws, xs, True, True)
                    mm.then_inc(up_done, 1)
                if s := at(LDOWN):
                    c, k, r = s
                    g = c * HT + k
                    first = isinstance(k, int) and k == 0
                    if first:
                        wait(pe, out_a, c)
                        wait(pe, out_b, c)
                    pe.wait_ge(h_low, g + 1)
                    pe.wait_ge(down_low, g + 1)
                    for t in range(4):
                        hs = [tuple(h[:, r, q, t * P:(t + 1) * P] for q in range(2))]
                        mm = split_matmul(pe, o_ps[t // 2][:, (t % 2) * D:(t % 2 + 1) * D], hs, [(down[:, r, 0, :], down[:, r, 1, :])],
                                          first and t % 2 == 0, isinstance(k, int) and k == HT - 1)
                    mm.then_inc(down_done, 1)
            steps(pe, step)


def mixture(nc, m):
    with ExitStack() as ctx:
        m.xt = ctx.enter_context(nc.sbuf_tensor("xt1", [P, 2, KT, N], F32R))
        e = dict(
            raw=ctx.enter_context(nc.sbuf_tensor("experts_raw", [P, HT * TILE], F32)),
            sel=ctx.enter_context(nc.sbuf_tensor("sel", [96, NRT * P], BF16)),
            pt=ctx.enter_context(nc.sbuf_tensor("probs_t", [96, N], BF16)),
        )
        weights_in = semaphore(nc, ctx, "weights_in")
        norm_transpose(nc, m, "n1", prefetch=lambda sp: load_tiles(sp, m, e, weights_in, 0, 6))
        router(nc, m, e)
        experts(nc, m, e, weights_in)


HALF = HEADS1 // 2
STACK = 3 * HD + 2


def windowed_projections(nc, m, a):
    with ExitStack() as ctx:
        def sb(name, shape, dt=F32):
            return ctx.enter_context(nc.sbuf_tensor(name, shape, dt))

        def sem(name):
            return semaphore(nc, ctx, name)

        def bank(name):
            return ctx.enter_context(nc.psum_tensor(name, [P, 512], F32))

        qk = sb("wqk", [P, 2, 2, 2, 2, CH], F32R)
        shut = sb("wshut", [P, 2, T], F32R)
        raw = sb("qkv_raw", [P, 3 * KT * D])
        wqkv = sb("wqkv", [P, 2, 3, KT, D], F32R)
        bqk = sb("bqk", [P, 4])
        bv = sb("bv", [P, D])
        ones = sb("ones_block", [P, HALF + 2 * (P - HALF)])
        kflag = sb("kflag", [2, T])
        square = sb("square", [P, 2, 2, CH])
        norms = sb("norms", [P, T + 2])
        best = sb("nbest", [P, 8])
        open_ = sb("open", [P, T])
        qk_ps = [bank(f"qk_ps{k}") for k in range(4)]
        v_ps = [bank("v_ps0"), bank("v_ps1")]
        n_ps = bank("n_ps")
        small, w_in, w_split = sem("wsmall"), sem("wqkv_in"), sem("wqkv_split")
        qk_done, v_done, high, low, v_out, squared, norm_step, norm_done = (
            sem("wqk_done"), sem("wv_done"), sem("whigh"), sem("wlow"), sem("wv_out"), sem("wsquared"), sem("wnorm_step"),
            sem("wnorm_done"))
        chain, ready, qk_stored, qk_free = sem("wchain"), sem("wready"), sem("wqk_stored"), sem("wqk_free")
        block = ctx.enter_context(nc.Block())

        @block.sync
        def _(sp):
            sp.dma_start(raw[:, :], m.io["wqkv"]).then_inc(w_in, 16)
            for dst, name in ((bqk[:, :], "bqk"), (bv[:, :], "bv"), (ones[:, :], "ones"), (kflag[:, :], "kflag")):
                sp.dma_start(dst, m.io[name]).then_inc(small, 16)
            for c in range(NCH):
                sp.wait_ge(low, 4 * c + 4)
                for of in range(2):
                    for part in range(2):
                        sp.dma_start(m.io["qk_scratch"][of, part, :, :, c * CH:(c + 1) * CH].rearrange("f p t -> p f t"),
                                     qk[:, c % 2, of, part, :, :].bitcast(F32)).then_inc(qk_stored, 16)
                if c % 2:
                    sp.wait_ge(qk_stored, 64 * (c + 1))
                    sp.sem_inc(qk_free, 1)
            sp.wait_ge(ready, 5)
            sp.dma_start(m.io["open_scratch"], shut[:, :, :].bitcast(F32)).then_inc(qk_stored, 16)
            sp.wait_ge(qk_stored, 64 * NCH + 16)

        @block.scalar
        def _(act):
            act.wait_ge(w_in, 16)
            act.copy(wqkv[:, 0].rearrange("p a k n -> p (a k n)"), raw[:, :]).then_inc(w_split, 1)
            act.wait_ge(small, 64)
            act.copy(a["kflag"][:, :], kflag[:, :]).then_inc(ready, 1)
            for c in range(NCH):
                if c == 2:
                    act.wait_ge(qk_free, 1)
                for j in range(4):
                    act.wait_ge(qk_done, 4 * c + j + 1)
                    act.activation(qk[:, c % 2, j // 2, 0, j % 2, :], qk_ps[j][:, :], ACT.Identity,
                                   bias=bqk[:, j:j + 1]).then_inc(high, 1)
                    if j < 2:
                        wait(act, norm_step, 4 * (c - 1))
                        act.activation(square[:, c % 2, j, :], qk_ps[j][:, :], ACT.Square, bias=bqk[:, j:j + 1]).then_inc(squared, 1)

        @block.vector
        def _(dve):
            dve.wait_ge(w_split, 1)
            dve.tensor_tensor(wqkv[:, 1].rearrange("p a k n -> p (a k n)"), raw[:, :],
                              wqkv[:, 0].rearrange("p a k n -> p (a k n)").bitcast(F32), ALU.subtract).then_inc(w_split, 1)
            dve.wait_ge(small, 64)
            for c in range(NCH):
                at = slice(c * CH, (c + 1) * CH)
                for j in range(4):
                    dve.wait_ge(high, 4 * c + j + 1)
                    if j < 2:
                        dve.wait_ge(squared, 2 * c + j + 1)
                    dve.scalar_tensor_tensor(out=qk[:, c % 2, j // 2, 1, j % 2, :], in0=qk_ps[j][:, :], scalar=bqk[:, j:j + 1],
                                             in1=qk[:, c % 2, j // 2, 0, j % 2, :].bitcast(F32),
                                             op0=ALU.add, op1=ALU.subtract).then_inc(low, 1)
                for k in range(2):
                    dve.wait_ge(v_done, 2 * c + k + 1)
                    for u in range(2):
                        t = 4 * c + 2 * k + u
                        ins = dve.tensor_tensor(a["v"][:, t * D:(t + 1) * D], v_ps[k][:, u * D:(u + 1) * D], bv[:, :], ALU.add)
                    ins.then_inc(v_out, 1)
            dve.memset(norms[:, T:T + 2], -2.0).then_inc(chain, 1)
            dve.wait_ge(norm_done, 1)
            dve.tensor_copy(norms[:, 0:T], n_ps[:, 0:T]).then_inc(chain, 1)
            n = 2
            for k in range(-(-NGLOBAL // 8)):
                dve.wait_ge(chain, n)
                dve.max(best[:, :], norms[:, 0:T]).then_inc(chain, 1)
                n += 1
                left = NGLOBAL - 8 * k
                if left < 8:
                    dve.wait_ge(chain, n)
                    dve.memset(best[:, left:8], -2.0).then_inc(chain, 1)
                    n += 1
                dve.wait_ge(chain, n)
                dve.match_replace(norms[:, :], best[:, :], norms[:, :], -1.0).then_inc(chain, 1)
                n += 1
            dve.wait_ge(chain, n)
            dve.tensor_scalar(open_[:, :], norms[:, 0:T], -1.0, -1.0e30, ALU.not_equal, ALU.mult).then_inc(chain, 1)
            dve.wait_ge(chain, n + 1)
            dve.memset(open_[:, 0:T:T - 1], 0.0).then_inc(chain, 1)
            dve.memset(norms[:, 0:T], 0.0).then_inc(chain, 1)
            dve.wait_ge(chain, n + 3)
            for k in range(2):
                own = slice(k * P, k * P + P)
                other = slice(P - k * P, 2 * P - k * P)
                dve.tensor_copy(shut[:, k, own], open_[:, own]).then_inc(ready, 1)
                dve.tensor_copy(shut[:, k, other], norms[:, other]).then_inc(ready, 1)

        @block.tensor
        def _(pe):
            def norm(c):
                pe.wait_ge(squared, 2 * c + 2)
                pe.wait_ge(small, 64)
                for s in range(2):
                    for j in range(2):
                        first = (2 * c + s) * HEADS1 + j * HALF
                        pe.matmul(n_ps[:, 0:T], ones[:, P - HALF - first:2 * P - HALF - first], square[:, c % 2, j, s * T:(s + 1) * T],
                                  start=c == 0 and s == 0 and j == 0, stop=c == NCH - 1 and s == 1 and j == 1
                                  ).then_inc(norm_step, 1)

            pe.wait_ge(w_split, 2)
            for c in range(NCH):
                at = slice(c * CH, (c + 1) * CH)
                for j in range(4):
                    wait(pe, low, 4 * (c - 1) + j + 1)
                    if j < 2:
                        wait(pe, squared, 2 * (c - 1) + j + 1)
                    ws = [tuple(wqkv[:, q, j // 2, k, (j % 2) * P:(j % 2 + 1) * P] for q in range(2)) for k in range(KT)]
                    split_matmul(pe, qk_ps[j][:, :], ws, [(m.xt[:, 0, k, at], m.xt[:, 1, k, at]) for k in range(KT)],
                                 True, True).then_inc(qk_done, 1)
                for k in range(2):
                    wait(pe, v_out, 2 * (c - 1) + k + 1)
                    for u in range(2):
                        t = 4 * c + 2 * k + u
                        xs = [tuple(m.xt[:, q, kt, t * P:(t + 1) * P] for q in range(2)) for kt in range(KT)]
                        mm = split_matmul(pe, v_ps[k][:, u * D:(u + 1) * D], xs,
                                          [(wqkv[:, 0, 2, kt, :], wqkv[:, 1, 2, kt, :]) for kt in range(KT)], True, True)
                    mm.then_inc(v_done, 1)
                if c >= 1:
                    norm(c - 1)
            norm(NCH - 1)
            pe.wait_ge(norm_step, 4 * NCH)
            pe.sem_inc(norm_done, 1)


def windowed_heads(nc, m, a):
    PAIRS = HEADS1 // 2
    QUAD = PAIRS // 2
    SCALE = HD ** -0.5
    LS, LEXP, LT, LV, LCOPY, LTURN, LOUT = 0, 1, 2, 3, 4, 5, 6
    LOADS = 7
    with ExitStack() as ctx:
        def sb(name, shape, dt=F32):
            return ctx.enter_context(nc.sbuf_tensor(name, shape, dt))

        def sem(name):
            return semaphore(nc, ctx, name)

        qs = sb("q_stack", [STACK, HEADS1, T], F32R)
        ks = sb("k_stack", [STACK, HEADS1, T], F32R)
        probs = sb("wprobs", [P, 2, 4 * T])
        top = sb("wtop", [P, 2, 4])
        neg = sb("wneg", [P, 2, 4])
        pt = sb("wpt", [P, 2, 2, 2 * T])
        alone = sb("values_alone", [P, 2, 2, HALF * (P + HD)])
        total = sb("wtotal", [P, 2, 2, HALF])
        inv = sb("winv", [P, 2, 2, HALF])
        context = sb("wcontext", [P, 2, T])
        s_ps = [ctx.enter_context(nc.psum_tensor(f"ws_ps{k}", [P, 4, T], F32)) for k in range(2)]
        t_ps = [ctx.enter_context(nc.psum_tensor(f"wt_ps{k}", [P, 2 * T], F32)) for k in range(2)]
        o_ps = [ctx.enter_context(nc.psum_tensor(f"wo_ps{k}", [P, 2, T], F32)) for k in range(2)]
        flags_in = sem("flags_in")
        stack_in = [sem("stack_in0"), sem("stack_in1")]
        s_done, neg_ready, exp_ready, t_done, pt_ready, o_done = (
            sem("ws_done"), sem("wneg_ready"), sem("wexp_ready"), sem("wt_done"), [sem("wpt0"), sem("wpt1")], sem("wo_done"))
        top_ready, cleared, alone_ready, inv_ready, context_ready, back_done, o_out, pause = (
            sem("wtop_ready"), sem("wcleared"), sem("walone_ready"), sem("winv_ready"), sem("wcontext_ready"),
            sem("wback_done"), sem("wo_out"), sem("wpause"))
        block = ctx.enter_context(nc.Block())

        def steps(eng, body):
            lagged_steps(eng, NSEQ, PAIRS, LOUT, body)

        def ends_half(s):
            return s and s[1] % QUAD == QUAD - 1

        @block.sync
        def _(sp):
            for h in range(HEADS1):
                sp.dma_start(ks[3 * HD:STACK, h, :].bitcast(F32), a["kflag"][:, :].bitcast(F32)).then_inc(flags_in, 16)

            def load(n, half):
                at = ds(n * T, T)
                hs = slice(half * HALF, (half + 1) * HALF)
                for i, (dst, of, order) in enumerate(((qs, 0, (0, 1, 0)), (ks, 1, (0, 0, 1)))):
                    for j, part in enumerate(order):
                        sp.dma_start(dst[j * HD:(j + 1) * HD, hs, :].bitcast(F32),
                                     m.io["qk_scratch"][of, part, half, :, at].rearrange("(h d) t -> d h t", h=HALF)
                                     ).then_inc(stack_in[half], 16)
                sp.dma_start(qs[3 * HD:STACK, hs, :].bitcast(F32),
                             m.io["open_scratch"][ds(n * HEADS1 + half * HALF, HALF), :, :].rearrange("h k t -> k h t")
                             ).then_inc(stack_in[half], 16)

            for half in range(2):
                load(0, half)
            with sp.Fori(1, NSEQ) as n:
                for half in range(2):
                    sp.wait_ge(s_done, n * PAIRS - PAIRS + (half + 1) * QUAD)
                    load(n, half)

        @block.gpsimd
        def _(pool):
            pool.memset(alone[:, :, :, :], 0.0).then_inc(cleared, 1)
            pool.wait_ge(cleared, 1)

            def values(n, half):
                src = a["v"][:, ds(n * 2 * D, 2 * D)].rearrange("p (k f h d) -> p k f h d", k=2, f=2, h=HALF)
                pool.tensor_copy(alone[:, half, :, :].rearrange("p k (h d) -> p k h d", h=HALF)[:, :, :, 0:HD],
                                 src[:, :, half, :, :]).then_inc(alone_ready, 1)

            for half in range(2):
                values(0, half)
            with pool.Fori(1, NSEQ) as n:
                for half in range(2):
                    pool.wait_ge(o_done, n * PAIRS - PAIRS + (half + 1) * QUAD)
                    pool.sem_inc(pause, 1)
                    values(n, half)

        @block.tensor
        def _(pe):
            pe.wait_ge(flags_in, 16 * HEADS1)

            def step(at):
                if s := at(LS):
                    n, j = s
                    g = n * PAIRS + j
                    if j % QUAD == 0:
                        pe.wait_ge(stack_in[j // QUAD], n * (16 * LOADS) + 16 * LOADS)
                    wait(pe, exp_ready, g - 1)
                    for u in range(2):
                        for t in range(2):
                            mm = pe.matmul(s_ps[j % 2][:, 2 * u + t, :], qs[:, 2 * j + u, t * P:(t + 1) * P], ks[:, 2 * j + u, :],
                                           start=True, stop=True)
                    mm.then_inc(s_done, 1)
                if s := at(LT):
                    n, j = s
                    g = n * PAIRS + j
                    pe.wait_ge(exp_ready, g + 1)
                    for u in range(2):
                        wait(pe, pt_ready[u], g)
                        for t in range(2):
                            for k in range(2):
                                mm = pe.transpose(t_ps[u][:, k * T + t * P:k * T + (t + 1) * P],
                                                  probs[:, j % 2, (2 * u + t) * T + k * P:(2 * u + t) * T + (k + 1) * P], m.ident[:, :])
                        mm.then_inc(t_done, 1)
                if s := at(LV):
                    n, j = s
                    g = n * PAIRS + j
                    half = j // QUAD
                    if j % QUAD == 0:
                        pe.wait_ge(alone_ready, n * 2 + half + 1)
                        wait(pe, o_out, n * 2 + half - 1)
                    for u in range(2):
                        pe.wait_ge(pt_ready[u], g + 1)
                        h = 2 * (j % QUAD) + u
                        for k in range(2):
                            mm = pe.matmul(o_ps[half][:, 0, :], alone[:, half, k, h * P:(h + 1) * P], pt[:, j % 2, u, k * T:(k + 1) * T],
                                           start=h == 0 and k == 0, stop=h == HALF - 1 and k == 1)
                    mm.then_inc(o_done, 1)
                if ends_half(s := at(LTURN)):
                    n, j = s
                    half = j // QUAD
                    pe.wait_ge(context_ready, n * 2 + half + 1)
                    for t in range(2):
                        mm = pe.transpose(o_ps[half][:, 1, t * P:(t + 1) * P], context[:, half, t * P:(t + 1) * P], m.ident[:, :])
                    mm.then_inc(back_done, 1)
            steps(pe, step)

        @block.scalar
        def _(act):
            def step(at):
                if s := at(LEXP):
                    n, j = s
                    g = n * PAIRS + j
                    half = j // QUAD
                    act.wait_ge(neg_ready, g + 1)
                    wait(act, t_done, 2 * g - 2)
                    if j % QUAD == 0:
                        wait(act, inv_ready, n * 2 + half - 1)
                    for u in range(2):
                        for t in range(2):
                            h = 2 * (j % QUAD) + u
                            ins = act.activation(probs[:, j % 2, (2 * u + t) * T:(2 * u + t + 1) * T], s_ps[j % 2][:, 2 * u + t, :],
                                                 ACT.Exp, bias=neg[:, j % 2, 2 * u + t:2 * u + t + 1], scale=SCALE,
                                                 accum_out=total[:, half, t, h:h + 1])
                    ins.then_inc(exp_ready, 1)
                if ends_half(s := at(LCOPY)):
                    n, j = s
                    half = j // QUAD
                    act.wait_ge(o_done, n * PAIRS + j + 1)
                    act.copy(context[:, half, :], o_ps[half][:, 0, :]).then_inc(context_ready, 1)
                if s := at(LT):
                    n, j = s
                    g = n * PAIRS + j
                    act.wait_ge(t_done, 2 * g + 1)
                    wait(act, o_done, g - 1)
                    act.copy(pt[:, j % 2, 0, :], t_ps[0][:, :]).then_inc(pt_ready[0], 1)
            steps(act, step)

        @block.vector
        def _(dve):
            def step(at):
                if s := at(LS):
                    n, j = s
                    g = n * PAIRS + j
                    dve.wait_ge(s_done, g + 1)
                    dve.tensor_reduce(top[:, j % 2, :], s_ps[j % 2][:, :, :], AX.X, ALU.max).then_inc(top_ready, 1)
                    wait(dve, exp_ready, g - 1)
                    dve.wait_ge(top_ready, g + 1)
                    dve.tensor_scalar(neg[:, j % 2, :], top[:, j % 2, :], -SCALE, None, ALU.mult).then_inc(neg_ready, 1)
                if s := at(LT):
                    n, j = s
                    g = n * PAIRS + j
                    dve.wait_ge(t_done, 2 * g + 2)
                    wait(dve, o_done, g - 1)
                    dve.tensor_copy(pt[:, j % 2, 1, :], t_ps[1][:, :]).then_inc(pt_ready[1], 1)
                if ends_half(s := at(LV)):
                    n, j = s
                    half = j // QUAD
                    dve.wait_ge(exp_ready, n * PAIRS + j + 1)
                    wait(dve, o_out, n * 2 + half - 1)
                    dve.reciprocal(inv[:, half, :, :], total[:, half, :, :]).then_inc(inv_ready, 1)
                if ends_half(s := at(LOUT)):
                    n, j = s
                    half = j // QUAD
                    dve.wait_ge(back_done, n * 2 + half + 1)
                    dve.wait_ge(inv_ready, n * 2 + half + 1)
                    dve.tensor_tensor(m.branch[:, ds(n * 2 * D, 2 * D)].rearrange("p (t f h d) -> p t f h d", t=2, f=2, h=HALF)[:, :, half],
                                      o_ps[half][:, 1, :].rearrange("p (t h d) -> p t h d", t=2, h=HALF),
                                      inv[:, half, :, :].rearrange("p t (h o) -> p t h o", o=1).to_broadcast([P, 2, HALF, HD]),
                                      ALU.mult).then_inc(o_out, 1)
            steps(dve, step)


def windowed_attention(nc, m):
    with ExitStack() as ctx:
        def sb(name, shape, dt=F32):
            return ctx.enter_context(nc.sbuf_tensor(name, shape, dt))

        a = dict(
            v=sb("wv", [P, NT * D]),
            kflag=sb("wkflag", [2, T], F32R),
        )
        with ExitStack() as inner:
            m.xt = inner.enter_context(nc.sbuf_tensor("xt2", [P, 2, KT, N], F32R))
            norm_transpose(nc, m, "n2")
            windowed_projections(nc, m, a)
        windowed_heads(nc, m, a)


def quantised_feed_forward(nc, m):
    ZERO = 128.0
    LUP, LHID, LDOWN, LOUT = 0, 1, 2, 3
    UP = KT * HIDT * P
    with ExitStack() as ctx:
        def sb(name, shape, dt=F32):
            return ctx.enter_context(nc.sbuf_tensor(name, shape, dt))

        def sem(name):
            return semaphore(nc, ctx, name)

        def bank(name):
            return ctx.enter_context(nc.psum_tensor(name, [P, 512], F32))

        m.xt = sb("xt3", [P, 2, KT, N], F32R)
        norm_transpose(nc, m, "n3")
        codes = sb("codes", [P, 2 * UP + HIDT * D], I32)
        wts = sb("qweights", [P, 2 * UP + HIDT * D], F32R)
        scales = sb("qscales", [P, 2 * HIDT])
        s_down = sb("s_down", [P, D])
        gated = sb("qgated", [P, 2, CH])
        hid = sb("qhid", [P, 2, CH])
        h = sb("qh", [P, 2, 2, CH], F32R)
        gate_ps, up_ps, o_ps = [[bank(f"{n}{k}") for k in range(2)] for n in ("qg_ps", "qu_ps", "qo_ps")]
        small, codes_in, wts_ready = sem("qsmall"), sem("codes_in"), sem("wts_ready")
        up_done, gated_ready, hid_ready, h_high, h_low, down_done, o_out = (
            sem("qup_done"), sem("qgated_ready"), sem("qhid_ready"), sem("qh_high"), sem("qh_low"), sem("qdown_done"), sem("qo_out"))
        block = ctx.enter_context(nc.Block())

        def steps(eng, body):
            lagged_steps(eng, NCH, HIDT, LOUT, body)

        @block.sync
        def _(sp):
            sp.dma_start(codes[:, :], m.io["codes"]).then_inc(codes_in, 16)
            sp.dma_start(scales[:, :], m.io["scales"]).then_inc(small, 16)
            sp.dma_start(s_down[:, :], m.io["s_down"]).then_inc(small, 16)

        @block.scalar
        def _(act):
            act.wait_ge(small, 32)

            def step(at):
                if s := at(LUP):
                    c, k = s
                    g = c * HIDT + k
                    act.wait_ge(up_done, g + 1)
                    wait(act, hid_ready, g - 1)
                    act.activation(gated[:, k % 2, :], gate_ps[k % 2][:, :], ACT.Silu, scale=scales[:, k:k + 1]).then_inc(gated_ready, 1)
                if s := at(LHID):
                    c, k = s
                    g = c * HIDT + k
                    act.wait_ge(hid_ready, g + 1)
                    wait(act, down_done, g - 1)
                    act.copy(h[:, k % 2, 0, :], hid[:, k % 2, :]).then_inc(h_high, 1)
            steps(act, step)

        @block.vector
        def _(dve):
            dve.wait_ge(codes_in, 16)
            dve.tensor_scalar(wts[:, :], codes[:, :], ZERO, None, ALU.subtract).then_inc(wts_ready, 1)
            dve.wait_ge(small, 32)

            def step(at):
                if s := at(LUP):
                    c, k = s
                    g = c * HIDT + k
                    dve.wait_ge(gated_ready, g + 1)
                    wait(dve, h_low, g - 1)
                    dve.scalar_tensor_tensor(out=hid[:, k % 2, :], in0=up_ps[k % 2][:, :], scalar=scales[:, HIDT + k:HIDT + k + 1],
                                             in1=gated[:, k % 2, :], op0=ALU.mult, op1=ALU.mult).then_inc(hid_ready, 1)
                if s := at(LHID):
                    c, k = s
                    g = c * HIDT + k
                    dve.wait_ge(h_high, g + 1)
                    dve.tensor_tensor(h[:, k % 2, 1, :], hid[:, k % 2, :], h[:, k % 2, 0, :].bitcast(F32), ALU.subtract).then_inc(h_low, 1)
                if s := at(LDOWN):
                    c, k = s
                    if k == HIDT - 1:
                        dve.wait_ge(down_done, (c + 1) * HIDT)
                        for t in range(2):
                            ins = dve.tensor_tensor(m.branch[:, ds(c * 4 * D + t * 2 * D, 2 * D)].rearrange("p (u d) -> p u d", u=2),
                                                    o_ps[t][:, :].rearrange("p (u d) -> p u d", u=2),
                                                    s_down[:, :].rearrange("p (u d) -> p u d", u=1).to_broadcast([P, 2, D]), ALU.mult)
                        ins.then_inc(o_out, 1)
            steps(dve, step)

        @block.tensor
        def _(pe):
            pe.wait_ge(wts_ready, 1)

            def step(at):
                if s := at(LUP):
                    c, k = s
                    g = c * HIDT + k
                    wait(pe, hid_ready, g - 1)
                    for o, base in ((gate_ps, 0), (up_ps, UP)):
                        for kt in range(KT):
                            for part in range(2):
                                mm = pe.matmul(o[k % 2][:, :], wts[:, base + (kt * HIDT + k) * P:base + (kt * HIDT + k + 1) * P],
                                               m.xt[:, part, kt, ds(c * CH, CH)], start=kt == 0 and part == 0,
                                               stop=kt == KT - 1 and part == 1)
                    mm.then_inc(up_done, 1)
                if s := at(LDOWN):
                    c, k = s
                    g = c * HIDT + k
                    if k == 0:
                        wait(pe, o_out, c)
                    pe.wait_ge(h_low, g + 1)
                    for t in range(4):
                        for part in range(2):
                            mm = pe.matmul(o_ps[t // 2][:, (t % 2) * D:(t % 2 + 1) * D], h[:, k % 2, part, t * P:(t + 1) * P],
                                           wts[:, 2 * UP + k * D:2 * UP + (k + 1) * D], start=k == 0 and part == 0 and t % 2 == 0,
                                           stop=k == HIDT - 1 and part == 1, skip_group_check=True)
                    mm.then_inc(down_done, 1)
            steps(pe, step)


def program(nc, io, upto=99):
    with ExitStack() as ctx:
        m = Memory(nc, ctx, io)
        with ExitStack() as inner:
            m.xt = inner.enter_context(nc.sbuf_tensor("xt0", [P, 2, KT, N], F32R))
            norm_transpose(nc, m, "n0", first=True)
            latent_attention(nc, m)
        if upto == 1:
            return norm_transpose(nc, m, "n1", last=True)
        mixture(nc, m)
        if upto == 2:
            return norm_transpose(nc, m, "n2", last=True)
        windowed_attention(nc, m)
        if upto == 3:
            return norm_transpose(nc, m, "n3", last=True)
        quantised_feed_forward(nc, m)
        norm_transpose(nc, m, "n4", last=True)


def scratch(nc):
    return {
        "qk_scratch": nc.dram_tensor("qk_scratch", (2, 2, 2, P, N), F32, kind="Internal").ap(),
        "open_scratch": nc.dram_tensor("open_scratch", (P, 2, T), F32, kind="Internal").ap(),
    }


def layout(x):
    import numpy as np
    f = {k: np.asarray(v) for k, v in x.items()}
    turn = np.concatenate([np.arange(0, LAT, 2), np.arange(1, LAT, 2)])

    def rows(w):
        return np.ascontiguousarray(w.reshape(-1, P, w.shape[-1]).transpose(1, 0, 2).reshape(P, -1))

    def wide(v):
        return np.ascontiguousarray(np.broadcast_to(v, (P, v.shape[0])))

    ang = np.arange(T, dtype=np.float32)[:, None] * (
        np.float32(10000.0) ** (-np.arange(LAT // 2, dtype=np.float32) / np.float32(LAT // 2)))[None, :]
    cos, sin = np.cos(ang).T, np.sin(ang).T
    causal = np.where(np.arange(P)[:, None] >= np.arange(P)[None, :], np.float32(0), np.float32(LOWEST))
    heads = np.arange(HEADS0) * LAT
    pad = NSH * P - HE
    wide1, wide3 = (np.concatenate([f[f"L0_ffn_{w}_shared"], np.zeros((D, pad), np.float32),
                                    f[f"L0_ffn_{w}_routed"].transpose(1, 0, 2).reshape(D, NE * HE)], axis=1)
                    for w in ("w1", "w3"))
    tall2 = np.concatenate([f["L0_ffn_w2_shared"], np.zeros((pad, D), np.float32),
                            f["L0_ffn_w2_routed"].reshape(NE * HE, D)])
    ups = [w.reshape(KT, P, HT, P).transpose(1, 2, 0, 3).reshape(P, HT, KT * P) for w in (wide1, wide3)]
    tiles = np.concatenate([*ups, tall2.reshape(HT, P, D).transpose(1, 0, 2)], axis=2)
    ones = np.zeros((P, HALF + 2 * (P - HALF)), np.float32)
    ones[np.arange(P), P - HALF + np.arange(P) // HD] = 1
    kflag = np.stack([np.arange(T) >= P + P // 2, np.arange(T) < P // 2]).astype(np.float32)
    hpad = HIDT * P - HID
    codes = [np.pad(f["L1_ffn_wq_gate"].T, ((0, 0), (0, hpad)), constant_values=128),
             np.pad(f["L1_ffn_wq_up"].T, ((0, 0), (0, hpad)), constant_values=128),
             np.pad(f["L1_ffn_wq_down"].T, ((0, hpad), (0, 0)), constant_values=128)]
    scales = [np.pad(f[f"L1_ffn_s_{w}"], (0, hpad)) for w in ("gate", "up")]
    gate = np.zeros((D, P), np.float32)
    gate[:, :NE] = f["L0_ffn_gate_w"].T
    gb = np.zeros((P, 1), np.float32)
    gb[:NE, 0] = f["L0_ffn_gate_b"]
    sel = (np.arange(96)[:, None] % 32 == np.arange(NRT * P)[None, :] // HE)
    io = {
        "x": f["L0_attn_x"].reshape(N, D),
        "ident": np.eye(P, dtype=np.float32),
        "wl": rows(f["L0_attn_W_latent"][:, turn]),
        "bl": f["L0_attn_b_latent"][turn].reshape(P, 1),
        "wd": rows(f["L0_attn_W_d"][:, (heads[:, None] + turn[None]).ravel()]),
        "bd": np.ascontiguousarray(f["L0_attn_b_d"].reshape(HEADS0, LAT)[:, turn].T),
        "wp": rows(f["L0_attn_W_proj"][(heads[:, None] + turn[None]).ravel(), :]),
        "bproj": wide(f["L0_attn_b_proj"]),
        "trig": np.stack([np.concatenate([cos, cos]), np.concatenate([sin, -sin])], axis=1).astype(np.float32),
        "experts": tiles.reshape(P, HT * TILE),
        "gate": rows(gate), "gb": gb,
        "sel": sel.astype(np.float32),
        "wqkv": np.concatenate([rows(f[f"L1_attn_W{w}"]) for w in "qkv"], axis=1),
        "bqk": np.concatenate([f["L1_attn_bq"].reshape(2, P), f["L1_attn_bk"].reshape(2, P)]).T,
        "bv": wide(f["L1_attn_bv"]),
        "ones": ones, "kflag": kflag,
        "codes": np.concatenate([*(rows(c) for c in codes)], axis=1),
        "scales": np.concatenate([s.reshape(HIDT, P) for s in scales]).T,
        "s_down": wide(f["L1_ffn_s_down"]),
        "mask": np.concatenate([causal, np.zeros((P, P), np.float32), causal], axis=1),
    }
    return {k: np.ascontiguousarray(v) for k, v in io.items()}


def kernel(**inputs):
    import numpy as np
    from concourse import bacc
    from concourse.bass_utils import run_bass_kernel_spmd

    nc = bacc.Bacc("TRN2", target_bir_lowering=False, num_devices=1)
    arrays = layout(inputs)
    io = {k: nc.dram_tensor(f"in_{k}", a.shape, mybir.dt.from_np(a.dtype), kind="ExternalInput").ap()
          for k, a in arrays.items()}
    io |= scratch(nc)
    io["out"] = nc.dram_tensor("out_x", (N, D), F32, kind="ExternalOutput").ap()
    program(nc, io)
    r = run_bass_kernel_spmd(nc, [{f"in_{k}": a for k, a in arrays.items()}], core_ids=[0])
    return np.asarray(r.results[0]["out_x"]).reshape(NSEQ, T, D)
```

```python
from contextlib import ExitStack

import concourse.bass as bass
from concourse import mybir

F32 = mybir.dt.float32
F32R = mybir.dt.float32r
BF16 = mybir.dt.bfloat16
I32 = mybir.dt.int32
ALU = mybir.AluOpType
ACT = mybir.ActivationFunctionType
AX = mybir.AxisListType
ds = bass.ds

P = 128
NSEQ, T, D = 8, 256, 256
N = NSEQ * T
NT = N // P
KT = D // P
EPS = 1e-5
HEADS0, LAT = 16, 128
NE, TOPK, HE = 16, 4, 176
NSH = -(-HE // P)
NRT = NE * HE // P
HEADS1, HD = 16, 16
NGLOBAL = 62
HID = 704
HIDT = -(-HID // P)
LOWEST = -3.0e38
NOTE = 1.0e9


def semaphore(nc, ctx, name):
    s = ctx.enter_context(nc.semaphore(name))
    ctx.callback(nc.sync.sem_clear, s)
    return s


class Memory:

    def __init__(self, nc, ctx, io):
        def sb(name, shape, dt=F32):
            return ctx.enter_context(nc.sbuf_tensor(name, shape, dt))

        self.io = io
        self.x = sb("x_res", [P, NT * D])
        self.branch = sb("branch", [P, NT * D])
        self.xt = None
        self.ident = sb("ident", [P, P])
        self.half = sb("minus_half", [P, NT])
        self.rstd = sb("x_rstd", [P, NT])
        self.shift = sb("x_shift", [P, NT])


def wait(eng, s, value):
    if not isinstance(value, int) or value > 0:
        eng.wait_ge(s, value)


def norm_transpose(nc, m, tag, first=False, prefetch=None, aside={}):
    LSHIFT, LADD, LSTAT, LNORM, LSPLIT = (1, 2, 3, 4, 5) if not first else (0, 0, 0, 1, 3)
    LOADS = 4 if first else 0
    BRANCH, X = 0, 1
    with ExitStack() as ctx:
        def sb(name, shape, dt=F32):
            return ctx.enter_context(nc.sbuf_tensor(f"{tag}_{name}", shape, dt))

        def sem(name):
            return semaphore(nc, ctx, f"{tag}_{name}")

        stats = sb("stats", [P, 2, 2, 6])
        mv = sb("mv", [P, 2, NT, 2])
        ve = sb("ve", [P, 2, NT])
        minus_mean = sb("minus_mean", [P, 2, NT])
        rstd = sb("rstd", [P, 2, NT])
        shift = sb("shift", [P, 2, NT])
        normed = sb("normed", [P, 2, 2 * D])
        xn = sb("xn", [P, 2, 2 * D])
        turned = [ctx.enter_context(nc.psum_tensor(f"{tag}_turned{k}", [P, KT, T], F32)) for k in range(3)]
        loaded = [sem(f"loaded{k}") for k in range(LOADS)]
        consts = sem("consts")
        gap = sem("gap")
        moments = [sem("moments_b"), sem("moments_x")]
        rstd_ready = [sem("rstd_b"), sem("rstd_x")]
        shift_ready = [sem("shift_b"), sem("shift_x")]
        normed_ready = sem("normed_ready")
        xn_ready = sem("xn_ready")
        turned_ready = sem("turned_ready")
        high_ready = sem("high_ready")
        m.low_ready = low_ready = sem("low_ready")
        x_final = sem("x_final")
        block = ctx.enter_context(nc.Block())

        def steps(body, besides=None):
            for s in range(NSEQ + LSPLIT):
                body(lambda lag: s - lag if 0 <= s - lag < NSEQ else None)
                if besides:
                    besides(s)

        def pair(b):
            return slice(b * 2 * D, (b + 1) * 2 * D)

        if first:
            @block.sync
            def _(sp):
                sp.dma_start(m.ident[:, :], m.io["ident"]).then_inc(consts, 16)
                for k in range(LOADS):
                    n = NSEQ // LOADS
                    sp.dma_start(m.x[:, k * n * 2 * D:(k + 1) * n * 2 * D].rearrange("p (u d) -> p u d", u=2 * n),
                                 m.io["x"][k * n * T:(k + 1) * n * T, :].rearrange("(u p) d -> p u d", p=P)
                                 ).then_inc(loaded[k], 16)
        if prefetch:
            block.sync(prefetch)
        @block.gpsimd
        def _(pool):
            if first:
                pool.memset(m.half[:, :], -0.5).then_inc(x_final, 1)
                pool.wait_ge(x_final, 1)

            def factors(of, b):
                at = slice(2 * b, 2 * b + 2)
                pool.wait_ge(moments[of], b + 1)
                pool.tensor_tensor(rstd[:, of, at], ve[:, of, at], m.half[:, at], ALU.pow).then_inc(rstd_ready[of], 1)
                pool.wait_ge(rstd_ready[of], b + 1)
                pool.tensor_tensor(shift[:, of, at], minus_mean[:, of, at], rstd[:, of, at], ALU.mult).then_inc(shift_ready[of], 1)

            def step(at):
                if not first and (b := at(LADD)) is not None:
                    pool.wait_ge(normed_ready, b + 1)
                    pool.tensor_tensor(m.x[:, pair(b)], m.x[:, pair(b)], normed[:, b % 2, :], ALU.add).then_inc(x_final, 1)
                if not first and (b := at(0)) is not None:
                    factors(BRANCH, b)
                if (b := at(LSTAT)) is not None:
                    factors(X, b)
            steps(step, aside.get("pool"))

        @block.vector
        def _(dve):
            count = 0

            def step(at):
                nonlocal count
                todo = []
                if (b := at(LSTAT)) is not None:
                    if first:
                        dve.wait_ge(loaded[b * LOADS // NSEQ], 16)
                    else:
                        dve.wait_ge(x_final, b + 1)
                    todo.append((X, b, m.x))
                if not first and (b := at(0)) is not None:
                    todo.append((BRANCH, b, m.branch))
                for of, b, src in todo:
                    for u in range(2):
                        dve.bn_stats(stats[:, of, u, :], src[:, (2 * b + u) * D:(2 * b + u + 1) * D]).then_inc(gap, 1)
                        count += 1
                if todo:
                    dve.wait_ge(gap, count)
                for of, b, src in todo:
                    for u in range(2):
                        dve.bn_aggr(mv[:, of, 2 * b + u, :], stats[:, of, u, :]).then_inc(gap, 1)
                        count += 1
                if todo:
                    dve.wait_ge(gap, count)
                for of, b, src in todo:
                    both = slice(2 * b, 2 * b + 2)
                    dve.tensor_scalar(minus_mean[:, of, both], mv[:, of, both, 0], -1.0, None, ALU.mult)
                    dve.tensor_scalar(ve[:, of, both], mv[:, of, both, 1], EPS, None, ALU.add).then_inc(moments[of], 1)
                if (b := at(LSPLIT)) is not None:
                    dve.wait_ge(high_ready, b + 1)
                    tokens = slice(b * T, (b + 1) * T)
                    dve.tensor_tensor(m.xt[:, 1, :, tokens], turned[b % 3][:, :, :], m.xt[:, 0, :, tokens].bitcast(F32),
                                      ALU.subtract).then_inc(low_ready, 1)
            steps(step, aside.get("dve"))

        @block.scalar
        def _(act):
            def norm(of, b, out, src, ready):
                act.wait_ge(shift_ready[of], b + 1)
                for u in range(2):
                    t = 2 * b + u
                    ins = act.activation(out[:, b % 2, u * D:(u + 1) * D], src[:, t * D:(t + 1) * D], ACT.Identity,
                                         scale=rstd[:, of, t:t + 1], bias=shift[:, of, t:t + 1])
                ins.then_inc(ready, 1)

            def step(at):
                if not first and (b := at(LSHIFT)) is not None:
                    wait(act, x_final, b - 1)
                    norm(BRANCH, b, normed, m.branch, normed_ready)
                if (b := at(LSPLIT)) is not None:
                    act.wait_ge(turned_ready, b + 1)
                    act.copy(m.xt[:, 0, :, b * T:(b + 1) * T], turned[b % 3][:, :, :]).then_inc(high_ready, 1)
                if (b := at(LNORM)) is not None:
                    wait(act, turned_ready, b - 1)
                    norm(X, b, xn, m.x, xn_ready)
            steps(step, aside.get("act"))

        @block.tensor
        def _(pe):
            if first:
                pe.wait_ge(consts, 16)

            def step(at):
                if (b := at(LNORM)) is not None:
                    wait(pe, low_ready, b - 2)
                    pe.wait_ge(xn_ready, b + 1)
                    for u in range(2):
                        for k in range(KT):
                            mm = pe.transpose(turned[b % 3][:, k, u * P:(u + 1) * P],
                                              xn[:, b % 2, u * D + k * P:u * D + (k + 1) * P], m.ident[:, :])
                    mm.then_inc(turned_ready, 1)
            steps(step, aside.get("pe"))


def hold(eng, pause, s, value):
    eng.wait_ge(s, value)
    if not isinstance(value, int):
        eng.sem_inc(pause, 1)


class Residual:
    AHEAD = 2

    def __init__(self, nc, ctx, m, tag, ring):
        def sb(name, shape):
            return ctx.enter_context(nc.sbuf_tensor(f"{tag}_{name}", shape, F32))

        def sem(name):
            return semaphore(nc, ctx, f"{tag}_{name}")

        self.m, self.ring = m, ring
        self.stats = sb("stats", [P, 2, ring, 2, 6])
        self.mv = sb("mv", [P, 2, ring, 2, 2])
        self.ve = sb("ve", [P, 2, ring, 2])
        self.minus_mean = sb("minus_mean", [P, 2, ring, 2])
        self.rstd = sb("rstd", [P, ring, 2])
        self.shift = sb("shift", [P, ring, 2])
        self.normed = sb("normed", [P, ring, 2 * D])
        self.gap = [sem("gap_b"), sem("gap_x")]
        self.ready = [sem("moments_b"), sem("moments_x")]
        self.rstd_ready = [sem("rstd_b"), sem("rstd_x")]
        self.factors_ready = sem("factors_b")
        self.normed_ready = sem("normed_ready")
        self.x_final = sem("x_final")
        self.pause = [sem(f"pause_{e}") for e in ("dve", "pool", "act")]

    def final(self, b):
        return b + (1 + self.AHEAD)

    def start(self, pool):
        pool.sem_inc(self.x_final, self.AHEAD)

    def moments(self, dve, of, b, r, src, after, value):
        pause = self.pause[0]
        hold(dve, pause, self.x_final, self.final(b) - (0 if of else self.ring))
        hold(dve, pause, after, value)
        for u in range(2):
            dve.bn_stats(self.stats[:, of, r, u, :], src[:, ds(b * (2 * D) + u * D, D)]).then_inc(self.gap[of], 1)
        hold(dve, pause, self.gap[of], b * 4 + 2)
        for u in range(2):
            dve.bn_aggr(self.mv[:, of, r, u, :], self.stats[:, of, r, u, :]).then_inc(self.gap[of], 1)
        hold(dve, pause, self.gap[of], b * 4 + 4)
        dve.tensor_scalar(self.minus_mean[:, of, r, :], self.mv[:, of, r, :, 0], -1.0, None, ALU.mult)
        dve.tensor_scalar(self.ve[:, of, r, :], self.mv[:, of, r, :, 1], EPS, None, ALU.add).then_inc(self.ready[of], 1)

    def moments_branch(self, dve, b, r, after, value):
        self.moments(dve, 0, b, r, self.m.branch, after, value)

    def moments_x(self, dve, b, r):
        self.moments(dve, 1, b, r, self.m.x, self.x_final, self.final(b))

    def factors(self, pool, of, b, r):
        pause = self.pause[1]
        rstd, shift = (self.m.rstd[:, ds(b * 2, 2)], self.m.shift[:, ds(b * 2, 2)]) if of else (self.rstd[:, r, :], self.shift[:, r, :])
        hold(pool, pause, self.ready[of], b + 1)
        pool.tensor_tensor(rstd, self.ve[:, of, r, :], self.m.half[:, 0:2], ALU.pow).then_inc(self.rstd_ready[of], 1)
        hold(pool, pause, self.rstd_ready[of], b + 1)
        ins = pool.tensor_tensor(shift, self.minus_mean[:, of, r, :], rstd, ALU.mult)
        if not of:
            ins.then_inc(self.factors_ready, 1)

    def norm(self, act, b, r):
        hold(act, self.pause[2], self.factors_ready, b + 1)
        for u in range(2):
            ins = act.activation(self.normed[:, r, u * D:(u + 1) * D], self.m.branch[:, ds(b * (2 * D) + u * D, D)], ACT.Identity,
                                 scale=self.rstd[:, r, u:u + 1], bias=self.shift[:, r, u:u + 1])
        ins.then_inc(self.normed_ready, 1)

    def add(self, pool, b, r):
        hold(pool, self.pause[1], self.normed_ready, b + 1)
        at = ds(b * (2 * D), 2 * D)
        pool.tensor_tensor(self.m.x[:, at], self.m.x[:, at], self.normed[:, r, :], ALU.add).then_inc(self.x_final, 1)


def transpose_norm(nc, m, tag, prefetch, aside={}):
    with ExitStack() as ctx:
        def sem(name):
            return semaphore(nc, ctx, f"{tag}_{name}")

        xn = ctx.enter_context(nc.sbuf_tensor(f"{tag}_xn", [P, 3, 2 * D], F32))
        turned = [ctx.enter_context(nc.psum_tensor(f"{tag}_turned{k}", [P, KT, T], F32)) for k in range(4)]
        normed = [sem("normed0"), sem("normed1")]
        turned_ready, high_ready, low_ready = sem("turned_ready"), sem("high_ready"), sem("low_ready")
        block = ctx.enter_context(nc.Block())
        block.sync(prefetch)

        def steps(body, besides=None):
            for s in range(NSEQ + 2):
                body(lambda lag: s - lag if 0 <= s - lag < NSEQ else None)
                if besides:
                    besides(s)

        def tile(eng, b, u):
            wait(eng, turned_ready, b - 2)
            t = 2 * b + u
            return (xn[:, b % 3, u * D:(u + 1) * D], m.x[:, t * D:(t + 1) * D], m.rstd[:, t:t + 1], m.shift[:, t:t + 1])

        @block.scalar
        def _(act):
            def step(at):
                if (b := at(0)) is not None:
                    out, x, rstd, shift = tile(act, b, 0)
                    act.activation(out, x, ACT.Identity, scale=rstd, bias=shift).then_inc(normed[0], 1)
                if (b := at(2)) is not None:
                    act.wait_ge(turned_ready, b + 1)
                    act.copy(m.xt[:, 0, :, b * T:(b + 1) * T], turned[b % 4][:, :, :]).then_inc(high_ready, 1)
            steps(step, aside.get("act"))

        @block.vector
        def _(dve):
            def step(at):
                if (b := at(0)) is not None:
                    out, x, rstd, shift = tile(dve, b, 1)
                    dve.tensor_scalar(out, x, rstd, shift, ALU.mult, ALU.add).then_inc(normed[1], 1)
                if (b := at(2)) is not None:
                    dve.wait_ge(high_ready, b + 1)
                    tokens = slice(b * T, (b + 1) * T)
                    dve.tensor_tensor(m.xt[:, 1, :, tokens], turned[b % 4][:, :, :], m.xt[:, 0, :, tokens].bitcast(F32),
                                      ALU.subtract).then_inc(low_ready, 1)
            steps(step, aside.get("dve"))

        @block.tensor
        def _(pe):
            def step(at):
                if (b := at(0)) is not None:
                    wait(pe, low_ready, b - 3)
                    for u in range(2):
                        pe.wait_ge(normed[u], b + 1)
                        for k in range(KT):
                            mm = pe.transpose(turned[b % 4][:, k, u * P:(u + 1) * P],
                                              xn[:, b % 3, u * D + k * P:u * D + (k + 1) * P], m.ident[:, :])
                    mm.then_inc(turned_ready, 1)
            steps(step)


def lagged_steps(eng, rounds, width, most, body):
    def one_round(b):
        known = isinstance(b, int)
        for i in range(width if not (known and b == rounds) else most):
            def at(lag, i=i):
                if i >= lag:
                    return None if known and b == rounds else (b, i - lag)
                return None if known and b == 0 else (b - 1, i - lag + width)
            body(at)
    one_round(0)
    with eng.Fori(1, rounds) as b:
        one_round(b)
    one_round(rounds)


def split_matmul(pe, out, stationary, moving, start, stop):
    n = len(stationary)
    for k, ((sh, sl), (mh, ml)) in enumerate(zip(stationary, moving)):
        pe.matmul(out, sh, mh, start=start and k == 0, stop=False, skip_group_check=True)
        pe.matmul(out, sh, ml, start=False, stop=False, skip_group_check=True)
        mm = pe.matmul(out, sl, mh, start=False, stop=stop and k == n - 1, skip_group_check=True)
    return mm


def latent_attention(nc, m):
    with ExitStack() as ctx:
        def sb(name, shape, dt=F32):
            return ctx.enter_context(nc.sbuf_tensor(name, shape, dt))

        wd = sb("wd", [P, 2, KT * HEADS0 * LAT], F32R)
        wp = sb("wp", [P, 2, HEADS0 * D], F32R)
        krot = sb("krot", [P, 2, N], F32R)
        v32 = m.branch[:, :].rearrange("p (b n) -> p b n", b=NSEQ)[:, :, 0:2 * LAT]
        trig = sb("trig", [P, 2, T])
        bd = sb("bd", [P, HEADS0])
        mask = sb("mask", [P, 3 * P])
        bproj = sb("bproj", [P, D])
        w = dict(wd=wd, wp=wp, krot=krot, v32=v32, trig=trig, bd=bd, mask=mask, bproj=bproj)
        with ExitStack() as inner:
            w["wd_raw"] = inner.enter_context(nc.sbuf_tensor("wd_raw", [P, KT * HEADS0 * LAT], F32))
            w["wp_raw"] = inner.enter_context(nc.sbuf_tensor("wp_raw", [P, HEADS0 * D], F32))
            w["wl_raw"] = inner.enter_context(nc.sbuf_tensor("wl_raw", [P, KT * LAT], F32))
            w["bl"] = inner.enter_context(nc.sbuf_tensor("bl", [P, 1], F32))
            small, wd_in, wd_high, wd_low = (semaphore(nc, inner, n) for n in ("kv_small", "wd_in", "wd_high", "wd_low"))
            w["small"], w["wp_in"] = small, semaphore(nc, inner, "wp_in")
            PIECES, START = 4, 5

            def load(sp):
                for dst, name in ((w["wl_raw"][:, :], "wl"), (w["bl"][:, :], "bl"), (trig[:, :, :], "trig"), (bd[:, :], "bd"),
                                  (mask[:, :], "mask"), (bproj[:, :], "bproj")):
                    sp.dma_start(dst, m.io[name]).then_inc(small, 16)
                sp.dma_start(w["wd_raw"][:, :], m.io["wd"]).then_inc(wd_in, 16)
                sp.dma_start(w["wp_raw"][:, :], m.io["wp"]).then_inc(w["wp_in"], 16)

            def piece(s):
                n = KT * HEADS0 * LAT // PIECES
                return slice((s - START) * n, (s - START + 1) * n) if START <= s < START + PIECES else None

            def high(s):
                if at := piece(s):
                    nc.scalar.wait_ge(wd_in, 16)
                    nc.scalar.copy(wd[:, 0, at], w["wd_raw"][:, at]).then_inc(wd_high, 1)

            def low(s):
                if at := piece(s):
                    nc.gpsimd.wait_ge(wd_high, s - START + 1)
                    nc.gpsimd.tensor_tensor(wd[:, 1, at], w["wd_raw"][:, at], wd[:, 0, at].bitcast(F32), ALU.subtract).then_inc(wd_low, 1)

            norm_transpose(nc, m, "n0", first=True, prefetch=load, aside=dict(act=high, pool=low))
            latent_keys(nc, m, w)
        w["wd"] = wd[:, :, :].rearrange("p q (k n) -> p q k n", k=KT)
        w["wp"] = wp[:, :, :].rearrange("p q (h n) -> p q h n", h=HEADS0)
        latent_heads(nc, m, w)


def latent_keys(nc, m, w):
    with ExitStack() as ctx:
        def sb(name, shape, dt=F32):
            return ctx.enter_context(nc.sbuf_tensor(name, shape, dt))

        def sem(name):
            return semaphore(nc, ctx, name)

        CH = 512
        wp, raw, wl_raw, bl = w["wp"], w["wp_raw"], w["wl_raw"], w["bl"]
        small, wp_in = w["small"], w["wp_in"]
        wl = sb("wl", [P, 2, KT, LAT], F32R)
        kv = sb("kv", [P, 2, CH])
        rot = sb("k_rot", [P, 2, CH])
        part = sb("k_part", [P, CH])
        lat_ps = [ctx.enter_context(nc.psum_tensor(f"lat_ps{k}", [P, CH], F32)) for k in range(2)]
        val_ps = [ctx.enter_context(nc.psum_tensor(f"val_ps{k}", [P, CH], F32)) for k in range(2)]
        wl_split, wp_high, wp_low = sem("wl_split"), sem("wp_high"), sem("wp_low")
        lat_done, kv_ready, rot_chain, khigh, val_done, val_out = (sem("lat_done"), sem("kv_ready"), sem("rot_chain"),
                                                                   sem("khigh"), sem("val_done"), sem("val_out"))
        split_done, cos_done = sem("split_done"), sem("cos_done")
        block = ctx.enter_context(nc.Block())

        def piece(c):
            n = HEADS0 * D // 4
            return slice(c * n, (c + 1) * n)

        @block.gpsimd
        def _(pool):
            cos = w["trig"][:, 0:1, :].to_broadcast([P, 2, T])
            for c in range(4):
                pool.wait_ge(kv_ready, c + 1)
                wait(pool, split_done, c - 1)
                pool.tensor_tensor(rot[:, c % 2, :].rearrange("p (b t) -> p b t", b=2),
                                   kv[:, c % 2, :].rearrange("p (b t) -> p b t", b=2), cos, ALU.mult).then_inc(cos_done, 1)
                pool.wait_ge(wp_high, c + 1)
                pool.tensor_tensor(wp[:, 1, piece(c)], raw[:, piece(c)], wp[:, 0, piece(c)].bitcast(F32), ALU.subtract).then_inc(wp_low, 1)

        @block.scalar
        def _(act):
            act.wait_ge(small, 96)
            act.copy(wl[:, 0, :, :].rearrange("p k n -> p (k n)"), wl_raw[:, :]).then_inc(wl_split, 1)
            for c in range(4):
                act.wait_ge(lat_done, c + 1)
                if c >= 2:
                    act.wait_ge(val_done, c - 1)
                    act.wait_ge(rot_chain, 4 * (c - 2) + 3)
                act.activation(kv[:, c % 2, :], lat_ps[c % 2][:, :], ACT.Identity, bias=bl[:, 0:1]).then_inc(kv_ready, 1)
                act.wait_ge(wp_in, 16)
                act.copy(wp[:, 0, piece(c)], raw[:, piece(c)]).then_inc(wp_high, 1)
                act.wait_ge(rot_chain, 4 * c + 3)
                act.copy(w["krot"][:, 0, c * CH:(c + 1) * CH], rot[:, c % 2, :]).then_inc(khigh, 1)
                act.wait_ge(val_done, c + 1)
                act.copy(w["v32"][:, 2 * c:2 * c + 2, :], val_ps[c % 2][:, :].rearrange("p (b n) -> p b n", b=2)).then_inc(val_out, 1)

        @block.vector
        def _(dve):
            dve.wait_ge(small, 96)
            dve.wait_ge(wl_split, 1)
            dve.tensor_tensor(wl[:, 1, :, :].rearrange("p k n -> p (k n)"), wl_raw[:, :],
                              wl[:, 0, :, :].rearrange("p k n -> p (k n)").bitcast(F32),
                              ALU.subtract).then_inc(wl_split, 1)
            for c in range(4):
                dve.wait_ge(kv_ready, c + 1)
                src = kv[:, c % 2, :].rearrange("p (b t) -> p b t", b=2)
                prt = part[:, :].rearrange("p (b t) -> p b t", b=2)
                for a, z in ((0, 64), (64, 0)):
                    if c:
                        dve.wait_ge(rot_chain, 4 * c - 1)
                    dve.tensor_tensor(prt[a:a + 64], src[z:z + 64], w["trig"][z:z + 64, 1:2, :].to_broadcast([64, 2, T]),
                                      ALU.mult).then_inc(rot_chain, 1)
                dve.wait_ge(rot_chain, 4 * c + 2)
                dve.wait_ge(cos_done, c + 1)
                dve.tensor_tensor(rot[:, c % 2, :], rot[:, c % 2, :], part[:, :], ALU.add).then_inc(rot_chain, 1)
                dve.wait_ge(khigh, c + 1)
                dve.wait_ge(rot_chain, 4 * c + 3)
                dve.tensor_tensor(w["krot"][:, 1, c * CH:(c + 1) * CH], rot[:, c % 2, :],
                                  w["krot"][:, 0, c * CH:(c + 1) * CH].bitcast(F32), ALU.subtract).then_inc(split_done, 1)
                dve.wait_ge(split_done, c + 1)
                dve.sem_inc(rot_chain, 1)

        @block.tensor
        def _(pe):
            pe.wait_ge(wl_split, 2)

            def turn(c):
                pe.wait_ge(kv_ready, c + 1)
                if c >= 2:
                    pe.wait_ge(val_out, c - 1)
                for s in range(4):
                    mm = pe.transpose(val_ps[c % 2][:, s * P:(s + 1) * P], kv[:, c % 2, s * P:(s + 1) * P], m.ident[:, :])
                mm.then_inc(val_done, 1)

            for c in range(4):
                if c >= 2:
                    pe.wait_ge(kv_ready, c - 1)
                at = slice(c * CH, (c + 1) * CH)
                split_matmul(pe, lat_ps[c % 2][:, :], [(wl[:, 0, k, :], wl[:, 1, k, :]) for k in range(KT)],
                             [(m.xt[:, 0, k, at], m.xt[:, 1, k, at]) for k in range(KT)], True, True).then_inc(lat_done, 1)
                if c >= 1:
                    turn(c - 1)
            turn(3)


def latent_heads(nc, m, w):
    PAIRS = HEADS0 // 2
    SCALE = LAT ** -0.5
    LQ, LROT, LSUM, LS, LNORM, LT, LV, LO, LOUT = 0, 1, 2, 3, 4, 5, 6, 7, 8
    with ExitStack() as ctx:
        def sb(name, shape, dt=F32):
            return ctx.enter_context(nc.sbuf_tensor(name, shape, dt))

        def sem(name):
            return semaphore(nc, ctx, name)

        def bank(name):
            return ctx.enter_context(nc.psum_tensor(name, [P, 512], F32))

        qb = sb("qb", [P, 2, 2 * T])
        qsum = sb("qsum", [P, 2, 2 * T])
        qpart = sb("qpart", [P, 2 * T])
        qr = sb("qr", [P, 2, 2, 2 * T], F32R)
        probs = sb("probs0", [P, 4, 2, 3 * P])
        top = sb("top0", [P, 4, 4])
        neg = sb("neg0", [P, 4, 4])
        total = sb("total0", [P, 4, 4])
        inv = sb("inv0", [P, 4, 4])
        pt = sb("pt0", [P, 2, 2, 2, 3 * P], F32R)
        v = sb("v0", [P, 2, 2 * LAT], F32R)
        y = sb("y0", [P, 2, 2, 2 * T], F32R)
        q_ps, y_ps, o_ps = bank("q_ps"), bank("y_ps"), bank("o_ps")
        s_ps = [bank("s_ps0"), bank("s_ps1")]
        t_ps = [bank("t_ps0"), bank("t_ps1")]

        q_done, s_done, t_done, y_done, o_done = sem("q_done"), sem("s_done"), sem("t_done"), sem("y_done"), sem("o_done")
        qb_ready, qcos_ready, qpart_ready, qsum_ready, qhigh, qlow = (
            sem("qb_ready"), sem("qcos_ready"), sem("qpart_ready"), sem("qsum_ready"), sem("qhigh"), sem("qlow"))
        masked, neg_ready, exp_ready, inv_ready, probs_ready = (
            sem("masked"), sem("neg_ready"), sem("exp_ready"), sem("inv_ready"), sem("probs_ready"))
        phigh, plow, vhigh, vlow, yhigh, ylow, o_out = (
            sem("phigh"), sem("plow"), sem("vhigh"), sem("vlow"), sem("yhigh"), sem("ylow"), sem("o_out"))
        pause = sem("pause0")
        block = ctx.enter_context(nc.Block())

        def steps(eng, body):
            lagged_steps(eng, NSEQ, PAIRS, LOUT, body)

        @block.tensor
        def _(pe):
            def step(at):
                if s := at(LT):
                    b, j = s
                    g = b * PAIRS + j
                    r = j % 2
                    for u in range(2):
                        wait(pe, plow, g * 2 + u - 1)
                        pe.wait_ge(probs_ready, g * 2 + u + 1)
                        for k in range(3):
                            mm = pe.transpose(t_ps[u][:, k * P:(k + 1) * P], probs[:, j % 4, u, k * P:(k + 1) * P], m.ident[:, :])
                        mm.then_inc(t_done, 1)
                if s := at(LS):
                    b, j = s
                    g = b * PAIRS + j
                    r = j % 2
                    wait(pe, qlow, g + 1)
                    for u in range(2):
                        wait(pe, masked, g * 2 + u - 1)
                        for t, cols, keys in ((0, slice(0, P), P), (1, slice(P, 3 * P), 2 * P)):
                            q = [(qr[:, r, 0, u * T + t * P:u * T + t * P + P], qr[:, r, 1, u * T + t * P:u * T + t * P + P])]
                            kk = [(w["krot"][:, 0, ds(b * T, keys)], w["krot"][:, 1, ds(b * T, keys)])]
                            mm = split_matmul(pe, s_ps[u][:, cols], q, kk, True, True)
                        mm.then_inc(s_done, 1)
                if s := at(LV):
                    b, j = s
                    g = b * PAIRS + j
                    r = j % 2
                    wait(pe, ylow, g)
                    if j == 0:
                        wait(pe, vlow, b + 1)
                    pe.wait_ge(plow, g * 2 + 2)
                    split_matmul(pe, y_ps[:, :].rearrange("p (u t) -> p u t", u=2), [(v[:, 0, 0:LAT], v[:, 1, 0:LAT])],
                                 [(pt[:, r, 0, :, 0:2 * P], pt[:, r, 1, :, 0:2 * P])], True, False)
                    split_matmul(pe, y_ps[:, :].rearrange("p (u t) -> p u t", u=2)[:, :, P:T], [(v[:, 0, LAT:2 * LAT], v[:, 1, LAT:2 * LAT])],
                                 [(pt[:, r, 0, :, 2 * P:3 * P], pt[:, r, 1, :, 2 * P:3 * P])], False, True).then_inc(y_done, 1)
                if s := at(LQ):
                    b, j = s
                    g = b * PAIRS + j
                    wait(pe, qb_ready, g)
                    for u in range(2):
                        h = 2 * j + u
                        ws = [(w["wd"][:, 0, k, h * LAT:(h + 1) * LAT], w["wd"][:, 1, k, h * LAT:(h + 1) * LAT])
                              for k in range(KT)]
                        xs = [(m.xt[:, 0, k, ds(b * T, T)], m.xt[:, 1, k, ds(b * T, T)]) for k in range(KT)]
                        mm = split_matmul(pe, q_ps[:, u * T:(u + 1) * T], ws, xs, True, True)
                    mm.then_inc(q_done, 1)
                if s := at(LO):
                    b, j = s
                    g = b * PAIRS + j
                    r = j % 2
                    pe.wait_ge(ylow, g + 1)
                    if j == 0:
                        wait(pe, o_out, b)
                    for u in range(2):
                        for t in range(2):
                            ys = [(y[:, r, 0, u * T + t * P:u * T + t * P + P], y[:, r, 1, u * T + t * P:u * T + t * P + P])]
                            ws = [(w["wp"][:, 0, 2 * j + u, :], w["wp"][:, 1, 2 * j + u, :])]
                            mm = split_matmul(pe, o_ps[:, t * D:(t + 1) * D], ys, ws, j == 0 and u == 0 and t == 0,
                                              j == PAIRS - 1 and u == 1)
                    mm.then_inc(o_done, 1)
            steps(pe, step)

        @block.scalar
        def _(act):
            def step(at):
                if s := at(LROT):
                    b, j = s
                    g = b * PAIRS + j
                    r = j % 2
                    act.wait_ge(q_done, g + 1)
                    wait(act, qsum_ready, g - 1)
                    for u in range(2):
                        ins = act.activation(qb[:, r, u * T:(u + 1) * T], q_ps[:, u * T:(u + 1) * T], ACT.Identity,
                                             bias=w["bd"][:, 2 * j + u:2 * j + u + 1])
                    ins.then_inc(qb_ready, 1)
                if s := at(LSUM):
                    b, j = s
                    g = b * PAIRS + j
                    r = j % 2
                    act.wait_ge(qsum_ready, g + 1)
                    wait(act, s_done, g * 2 - 2)
                    act.copy(qr[:, r, 0, :], qsum[:, r, :]).then_inc(qhigh, 1)
                if s := at(LT):
                    b, j = s
                    g = b * PAIRS + j
                    r = j % 2
                    wait(act, y_done, g - 1)
                    for u in range(2):
                        act.wait_ge(t_done, g * 2 + u + 1)
                        act.copy(pt[:, r, 0, u, :], t_ps[u][:, 0:3 * P]).then_inc(phigh, 1)
                if s := at(LV):
                    b, j = s
                    g = b * PAIRS + j
                    r = j % 2
                    act.wait_ge(y_done, g + 1)
                    wait(act, o_done, g - 1)
                    act.copy(y[:, r, 0, :], y_ps[:, :]).then_inc(yhigh, 1)
                if s := at(LV - 1):
                    b, j = s
                    if j == 0:
                        wait(act, y_done, b * PAIRS)
                        act.sem_inc(pause, 1)
                        act.copy(v[:, 0, :], m.branch[:, ds(b * 2 * D, 2 * LAT)]).then_inc(vhigh, 1)
                if s := at(LS):
                    b, j = s
                    g = b * PAIRS + j
                    r = j % 2
                    act.wait_ge(neg_ready, g + 1)
                    for u in range(2):
                        for t, cols in ((0, slice(0, P)), (1, slice(P, 3 * P))):
                            ins = act.activation(probs[:, j % 4, u, cols], probs[:, j % 4, u, cols], ACT.Exp,
                                                 bias=neg[:, j % 4, 2 * u + t:2 * u + t + 1], scale=SCALE,
                                                 accum_out=total[:, j % 4, 2 * u + t:2 * u + t + 1])
                    ins.then_inc(exp_ready, 1)
            steps(act, step)

        @block.gpsimd
        def _(pool):
            cos = w["trig"][:, 0:1, :].to_broadcast([P, 2, T])

            def step(at):
                if s := at(LNORM):
                    b, j = s
                    g = b * PAIRS + j
                    pool.wait_ge(inv_ready, g + 1)
                    for t, cols, keys in ((0, slice(0, P), P), (1, slice(P, 3 * P), 2 * P)):
                        ins = pool.tensor_tensor(probs[:, j % 4, :, cols], probs[:, j % 4, :, cols],
                                                 inv[:, j % 4, t:4:2].rearrange("p (u o) -> p u o", o=1).to_broadcast([P, 2, keys]),
                                                 ALU.mult)
                    ins.then_inc(probs_ready, 2)
                if s := at(LSUM):
                    b, j = s
                    g = b * PAIRS + j
                    r = j % 2
                    pool.wait_ge(qhigh, g + 1)
                    pool.tensor_tensor(qr[:, r, 1, :], qsum[:, r, :], qr[:, r, 0, :].bitcast(F32), ALU.subtract).then_inc(qlow, 1)
                if s := at(LROT):
                    b, j = s
                    g = b * PAIRS + j
                    r = j % 2
                    wait(pool, qlow, g - 1)
                    pool.wait_ge(qb_ready, g + 1)
                    pool.tensor_tensor(qsum[:, r, :].rearrange("p (u t) -> p u t", u=2),
                                       qb[:, r, :].rearrange("p (u t) -> p u t", u=2), cos, ALU.mult).then_inc(qcos_ready, 1)
            steps(pool, step)

        @block.vector
        def _(dve):
            def step(at):
                if s := at(LNORM):
                    b, j = s
                    g = b * PAIRS + j
                    r = j % 2
                    dve.wait_ge(exp_ready, g + 1)
                    dve.reciprocal(inv[:, j % 4, :], total[:, j % 4, :]).then_inc(inv_ready, 1)
                if s := at(LSUM):
                    b, j = s
                    g = b * PAIRS + j
                    r = j % 2
                    dve.wait_ge(qcos_ready, g + 1)
                    dve.wait_ge(qpart_ready, g + 1)
                    dve.tensor_tensor(qsum[:, r, :], qsum[:, r, :], qpart[:, :], ALU.add).then_inc(qsum_ready, 1)
                if s := at(LS):
                    b, j = s
                    g = b * PAIRS + j
                    r = j % 2
                    wait(dve, t_done, g * 2 - 6)
                    for u in range(2):
                        dve.wait_ge(s_done, g * 2 + u + 1)
                        dve.sem_inc(pause, 1)
                        for t, cols in ((0, slice(0, P)), (1, slice(P, 3 * P))):
                            ins = dve.tensor_tensor_reduce(probs[:, j % 4, u, cols], s_ps[u][:, cols], w["mask"][:, cols],
                                                           1.0, LOWEST, ALU.add, ALU.max, top[:, j % 4, 2 * u + t:2 * u + t + 1])
                        ins.then_inc(masked, 1)
                    dve.wait_ge(masked, g * 2 + 2)
                    dve.tensor_scalar(neg[:, j % 4, :], top[:, j % 4, :], -SCALE, None, ALU.mult).then_inc(neg_ready, 1)
                if s := at(LOUT):
                    b, j = s
                    if j == PAIRS - 1:
                        dve.wait_ge(o_done, (b + 1) * PAIRS)
                        dve.tensor_tensor(m.branch[:, ds(b * 2 * D, 2 * D)].rearrange("p (u d) -> p u d", u=2),
                                          o_ps[:, :].rearrange("p (u d) -> p u d", u=2),
                                          w["bproj"][:, :].rearrange("p (u d) -> p u d", u=1).to_broadcast([P, 2, D]),
                                          ALU.add).then_inc(o_out, 1)
                if s := at(LT):
                    b, j = s
                    g = b * PAIRS + j
                    r = j % 2
                    for u in range(2):
                        dve.wait_ge(phigh, g * 2 + u + 1)
                        dve.tensor_tensor(pt[:, r, 1, u, :], t_ps[u][:, 0:3 * P], pt[:, r, 0, u, :].bitcast(F32),
                                          ALU.subtract).then_inc(plow, 1)
                if s := at(LV):
                    b, j = s
                    g = b * PAIRS + j
                    r = j % 2
                    dve.wait_ge(yhigh, g + 1)
                    dve.tensor_tensor(y[:, r, 1, :], y_ps[:, :], y[:, r, 0, :].bitcast(F32), ALU.subtract).then_inc(ylow, 1)
                if s := at(LROT):
                    b, j = s
                    g = b * PAIRS + j
                    r = j % 2
                    dve.wait_ge(qb_ready, g + 1)
                    wait(dve, qsum_ready, g)
                    for a, z in ((0, 64), (64, 0)):
                        ins = dve.tensor_tensor(qpart[a:a + 64, :].rearrange("p (u t) -> p u t", u=2),
                                                qb[z:z + 64, r, :].rearrange("p (u t) -> p u t", u=2),
                                                w["trig"][z:z + 64, 1:2, :].to_broadcast([64, 2, T]), ALU.mult)
                    ins.then_inc(qpart_ready, 1)
                if s := at(LV - 1):
                    b, j = s
                    if j == 0:
                        dve.wait_ge(vhigh, b + 1)
                        dve.tensor_tensor(v[:, 1, :], m.branch[:, ds(b * 2 * D, 2 * LAT)], v[:, 0, :].bitcast(F32),
                                          ALU.subtract).then_inc(vlow, 1)
            steps(dve, step)



HT = NSH + NRT
UPC = 2 * KT * P
TILE = UPC + D
CH = 512
NCH = N // CH


def load_tiles(sp, m, e, weights_in, a, z):
    for k in range(a, z):
        sp.dma_start(e["raw"][:, 2 * k * TILE:2 * (k + 1) * TILE], m.io["experts"][:, 2 * k * TILE:2 * (k + 1) * TILE]
                     ).then_inc(weights_in, 16)
        sp.wait_ge(weights_in, 16 * (k + 1))


def router(nc, m, e):
    with ExitStack() as ctx:
        def sb(name, shape, dt=F32):
            return ctx.enter_context(nc.sbuf_tensor(name, shape, dt))

        def sem(name):
            return semaphore(nc, ctx, name)

        WID = NE + TOPK
        gb, logits = e["gb"], e["logits"]
        sig = sb("sig", [P, NT, NE])
        score = sb("score", [P, NT, WID])
        best = sb("best", [P, NT, 8])
        found = sb("found", [P, NT, WID])
        prob = sb("prob", [P, NT, NE])
        total = sb("rtotal", [P, NT])
        parts = sb("pparts", [P, NT, 96], BF16)
        ident_b = sb("ident_b", [P, P], BF16)
        score_ps = ctx.enter_context(nc.psum_tensor("score_ps", [P, NT, NE], F32))
        pt_ps = [ctx.enter_context(nc.psum_tensor(f"pt_ps{k}", [P, CH], BF16)) for k in range(2)]
        exp_ready, score_done, ident_ready = sem("rexp_ready"), sem("score_done"), sem("ident_ready")
        chain, parts_ready, turned, out = sem("rchain"), sem("parts_ready"), sem("rturned"), sem("rout")
        block = ctx.enter_context(nc.Block())

        @block.scalar
        def _(act):
            e["copy_logits"](NSEQ - 1)
            act.copy(ident_b[:, :], m.ident[:, :]).then_inc(ident_ready, 1)
            act.wait_ge(score_done, 1)
            act.activation(sig[:, :, :], score_ps[:, :, :], ACT.Exp, scale=-1.0).then_inc(exp_ready, 1)
            act.copy(e["sel"][:, :], e["sel32"][:, :])

        @block.vector
        def _(dve):
            dve.memset(parts[:, :, :], 0.0).then_inc(parts_ready, 1)
            dve.memset(score[:, :, NE:WID], LOWEST).then_inc(parts_ready, 1)
            dve.wait_ge(exp_ready, 1)
            dve.tensor_scalar(sig[:, :, :], sig[:, :, :], 1.0, None, ALU.add).then_inc(exp_ready, 1)
            dve.wait_ge(exp_ready, 2)
            dve.reciprocal(sig[:, :, :], sig[:, :, :]).then_inc(exp_ready, 1)
            dve.wait_ge(exp_ready, 3)
            dve.tensor_tensor(score[:, :, 0:NE], sig[:, :, :],
                              gb[:, :].rearrange("p (o e) -> p o e", o=1).to_broadcast([P, NT, NE]), ALU.add).then_inc(chain, 1)
            dve.wait_ge(chain, 1)
            for t in range(NT):
                dve.max(best[:, t, :], score[:, t, 0:NE]).then_inc(chain, 1)
            dve.wait_ge(chain, 1 + NT)
            dve.memset(best[:, :, TOPK:8], LOWEST).then_inc(chain, 1)
            dve.wait_ge(chain, 2 + NT)
            for t in range(NT):
                dve.match_replace(found[:, t, :], best[:, t, :], score[:, t, :], 3.0e38).then_inc(chain, 1)
            dve.wait_ge(chain, 2 + 2 * NT)
            n = 2 + 2 * NT
            dve.tensor_tensor(prob[:, :, :], found[:, :, 0:NE], score[:, :, 0:NE], ALU.not_equal).then_inc(chain, 1)
            dve.wait_ge(chain, n + 1)
            dve.tensor_tensor(prob[:, :, :], prob[:, :, :], score[:, :, 0:NE], ALU.mult).then_inc(chain, 1)
            dve.wait_ge(chain, n + 2)
            dve.tensor_reduce(total[:, :], prob[:, :, :], AX.X, ALU.add).then_inc(chain, 1)
            dve.wait_ge(chain, n + 3)
            dve.reciprocal(total[:, :], total[:, :]).then_inc(chain, 1)
            dve.wait_ge(chain, n + 4)
            dve.tensor_tensor(prob[:, :, :], prob[:, :, :],
                              total[:, :].rearrange("p (t o) -> p t o", o=1).to_broadcast([P, NT, NE]), ALU.mult).then_inc(chain, 1)
            n += 5
            for k in range(3):
                dve.wait_ge(chain, n)
                dve.tensor_copy(parts[:, :, 32 * k:32 * k + NE], prob[:, :, :]).then_inc(chain, 1)
                if k < 2:
                    dve.wait_ge(chain, n + 1)
                    dve.tensor_tensor(prob[:, :, :], prob[:, :, :], parts[:, :, 32 * k:32 * k + NE], ALU.subtract).then_inc(chain, 1)
                n += 2
            dve.wait_ge(chain, n - 1)
            dve.sem_inc(parts_ready, 1)
            for c in range(NCH):
                dve.wait_ge(turned, c + 1)
                dve.tensor_copy(e["pt"][:, c * CH:(c + 1) * CH], pt_ps[c % 2][0:96, :]).then_inc(out, 1)

        @block.tensor
        def _(pe):
            for k in range(NT):
                if k == NT - 2:
                    pe.wait_ge(e["logits_ready"], NSEQ)
                mm = pe.transpose(score_ps[:, k, :], logits[:, k * P:(k + 1) * P], m.ident[0:NE, 0:NE])
            mm.then_inc(score_done, 1)
            pe.wait_ge(ident_ready, 1)
            pe.wait_ge(parts_ready, 3)
            for c in range(NCH):
                if c >= 2:
                    pe.wait_ge(out, c - 1)
                for s in range(4):
                    mm = pe.transpose(pt_ps[c % 2][0:96, s * P:(s + 1) * P], parts[:, 4 * c + s, :], ident_b[:, :])
                mm.then_inc(turned, 1)


def experts(nc, m, e, weights_in):
    HEAD = 8
    LSPLIT, LUP, LHID, LDOWN = 0, 1, 2, 3
    LBRANCH, LNORM, LSUM = 4, (5, 6), (6, 7)
    with ExitStack() as ctx:
        def sb(name, shape, dt=F32):
            return ctx.enter_context(nc.sbuf_tensor(name, shape, dt))

        def sem(name):
            return semaphore(nc, ctx, name)

        def bank(name):
            return ctx.enter_context(nc.psum_tensor(name, [P, CH], F32))

        raw = e["raw"]
        up = sb("up_w", [P, 2, 2, UPC], F32R)
        down = sb("down_w", [P, 2, 2, D], F32R)
        gated = sb("gated", [P, 2, CH])
        hid = sb("hid", [P, 2, CH])
        h = sb("h_parts", [P, 2, 2, CH], F32R)
        h1_ps = [bank("h1_ps0"), bank("h1_ps1")]
        h3_ps = [bank("h3_ps0"), bank("h3_ps1")]
        w_ps = bank("weight_ps")
        o_ps = [bank("eo_ps0"), bank("eo_ps1")]
        up_high, up_low, down_high, down_low = sem("up_high"), sem("up_low"), sem("down_high"), sem("down_low")
        up_done, weight_done, down_done = sem("up_done"), sem("weight_done"), sem("down_done")
        lifted, product_ready, silu_ready, hid_ready, h_high, h_low = (
            sem("lifted"), sem("product_ready"), sem("silu_ready"), sem("hid_ready"), sem("h_high"), sem("h_low"))
        out_a, out_b, pause = sem("eout_a"), sem("eout_b"), sem("epause")
        x = Residual(nc, ctx, m, "r1", 2)
        block = ctx.enter_context(nc.Block())

        def ends(s):
            return s and isinstance(s[1], int) and s[1] == HT - 1

        def steps(eng, body):
            def chunk(c):
                known = isinstance(c, int)
                for k in range(HEAD if not (known and c == NCH) else LSUM[1]):
                    def at(lag, k=k):
                        if k >= lag:
                            return None if known and c == NCH else (c, k - lag, (k - lag) % 2)
                        return None if known and c == 0 else (c - 1, k - lag + HT, (k - lag) % 2)
                    body(at)
                if known and c == NCH:
                    return
                with eng.Fori(0, (HT - HEAD) // 2) as it:
                    for o in range(2):
                        body(lambda lag, o=o: (c, it * 2 + (HEAD + o - lag), (HEAD + o - lag) % 2))
            chunk(0)
            with eng.Fori(1, NCH) as c:
                chunk(c)
            chunk(NCH)

        def shared(k):
            return isinstance(k, int) and k < NSH

        @block.sync
        def _(sp):
            load_tiles(sp, m, e, weights_in, 6, HT // 2)

        @block.scalar
        def _(act):
            def step(at):
                if s := at(LSPLIT):
                    c, k, r = s
                    act.wait_ge(weights_in, (k // 2) * 16 + 16 if isinstance(k, int) else k * 8 + (16 if r == 0 else 8))
                    wait(act, up_done, c * HT + k - 1)
                    act.sem_inc(pause, 1)
                    act.copy(up[:, r, 0, :], raw[:, ds(k * TILE, UPC)]).then_inc(up_high, 1)
                if s := at(LHID):
                    c, k, r = s
                    g = c * HT + k
                    if not shared(k):
                        act.wait_ge(product_ready, c * NRT + k - NSH + 1)
                        act.activation(gated[:, r, :], gated[:, r, :], ACT.Silu).then_inc(silu_ready, 1)
                    wait(act, down_done, g - 1)
                    act.sem_inc(pause, 1)
                    act.copy(down[:, r, 0, :], raw[:, ds(k * TILE + UPC, D)]).then_inc(down_high, 1)
                    act.wait_ge(hid_ready, g + 1)
                    act.copy(h[:, r, 0, :], hid[:, r, :]).then_inc(h_high, 1)
                if s := at(LUP):
                    c, k, r = s
                    g = c * HT + k
                    act.wait_ge(up_done, g + 1)
                    wait(act, hid_ready, g - 1)
                    if shared(k):
                        act.activation(gated[:, r, :], h1_ps[r][:, :], ACT.Silu).then_inc(lifted, 1)
                    else:
                        act.copy(gated[:, r, :], h3_ps[r][:, :]).then_inc(lifted, 1)
                if s := at(LDOWN):
                    c, k, r = s
                    if isinstance(k, int) and k == HT - 1:
                        act.wait_ge(down_done, (c + 1) * HT)
                        act.sem_inc(pause, 1)
                        act.copy(m.branch[:, ds(c * 4 * D, 2 * D)], o_ps[0][:, :]).then_inc(out_a, 1)
                for u in range(2):
                    if ends(s := at(LNORM[u])):
                        x.norm(act, s[0] * 2 + u, u)
            steps(act, step)

        @block.gpsimd
        def _(pool):
            x.start(pool)

            def step(at):
                if ends(s := at(LBRANCH)):
                    for u in range(2):
                        x.factors(pool, 0, s[0] * 2 + u, u)
                for u in range(2):
                    if ends(s := at(LNORM[u])):
                        x.add(pool, s[0] * 2 + u, u)
                for u in range(2):
                    if ends(s := at(LSUM[u])):
                        x.factors(pool, 1, s[0] * 2 + u, u)
            steps(pool, step)

        @block.vector
        def _(dve):
            def step(at):
                if s := at(LSPLIT):
                    c, k, r = s
                    g = c * HT + k
                    dve.wait_ge(up_high, g + 1)
                    dve.tensor_tensor(up[:, r, 1, :], raw[:, ds(k * TILE, UPC)], up[:, r, 0, :].bitcast(F32),
                                      ALU.subtract).then_inc(up_low, 1)
                if s := at(LHID):
                    c, k, r = s
                    g = c * HT + k
                    wait(dve, h_low, g - 1)
                    if shared(k):
                        dve.wait_ge(lifted, g + 1)
                        dve.tensor_tensor(hid[:, r, :], gated[:, r, :], h3_ps[r][:, :], ALU.mult).then_inc(hid_ready, 1)
                    else:
                        dve.wait_ge(silu_ready, c * NRT + k - NSH + 1)
                        dve.wait_ge(weight_done, c * NRT + k - NSH + 1)
                        dve.tensor_tensor(hid[:, r, :], gated[:, r, :], w_ps[:, :], ALU.mult).then_inc(hid_ready, 1)
                    dve.wait_ge(down_high, g + 1)
                    dve.tensor_tensor(down[:, r, 1, :], raw[:, ds(k * TILE + UPC, D)], down[:, r, 0, :].bitcast(F32),
                                      ALU.subtract).then_inc(down_low, 1)
                    dve.wait_ge(h_high, g + 1)
                    dve.tensor_tensor(h[:, r, 1, :], hid[:, r, :], h[:, r, 0, :].bitcast(F32), ALU.subtract).then_inc(h_low, 1)
                if s := at(LUP):
                    c, k, r = s
                    if not shared(k):
                        dve.wait_ge(lifted, c * HT + k + 1)
                        dve.tensor_tensor(gated[:, r, :], gated[:, r, :], h1_ps[r][:, :], ALU.mult).then_inc(product_ready, 1)
                if s := at(LDOWN):
                    c, k, r = s
                    if isinstance(k, int) and k == HT - 1:
                        dve.wait_ge(down_done, (c + 1) * HT)
                        dve.tensor_copy(m.branch[:, ds(c * 4 * D + 2 * D, 2 * D)], o_ps[1][:, :]).then_inc(out_b, 1)
                if ends(s := at(LBRANCH)):
                    for u in range(2):
                        x.moments_branch(dve, s[0] * 2 + u, u, (out_a, out_b)[u], s[0] + 1)
                for u in range(2):
                    if ends(s := at(LSUM[u])):
                        x.moments_x(dve, s[0] * 2 + u, u)
            steps(dve, step)

        @block.tensor
        def _(pe):
            def step(at):
                if s := at(LHID):
                    c, k, r = s
                    g = c * HT + k
                    if not shared(k):
                        wait(pe, hid_ready, g)
                        pe.matmul(w_ps[:, :], e["sel"][:, ds((k - NSH) * P, P)], e["pt"][:, ds(c * CH, CH)],
                                  start=True, stop=True).then_inc(weight_done, 1)
                if s := at(LUP):
                    c, k, r = s
                    g = c * HT + k
                    pe.wait_ge(up_low, g + 1)
                    wait(pe, hid_ready, g - 1)
                    xs = [(m.xt[:, 0, kt, ds(c * CH, CH)], m.xt[:, 1, kt, ds(c * CH, CH)]) for kt in range(KT)]
                    for j, o in ((1, h3_ps[r]), (0, h1_ps[r])):
                        ws = [tuple(up[:, r, q, (j * KT + kt) * P:(j * KT + kt + 1) * P] for q in range(2)) for kt in range(KT)]
                        mm = split_matmul(pe, o[:, :], ws, xs, True, True)
                    mm.then_inc(up_done, 1)
                if s := at(LDOWN):
                    c, k, r = s
                    g = c * HT + k
                    first = isinstance(k, int) and k == 0
                    if first:
                        wait(pe, out_a, c)
                        wait(pe, out_b, c)
                    pe.wait_ge(h_low, g + 1)
                    pe.wait_ge(down_low, g + 1)
                    for t in range(4):
                        hs = [tuple(h[:, r, q, t * P:(t + 1) * P] for q in range(2))]
                        mm = split_matmul(pe, o_ps[t // 2][:, (t % 2) * D:(t % 2 + 1) * D], hs, [(down[:, r, 0, :], down[:, r, 1, :])],
                                          first and t % 2 == 0, isinstance(k, int) and k == HT - 1)
                    mm.then_inc(down_done, 1)
            steps(pe, step)


def mixture(nc, m):
    with ExitStack() as ctx:
        m.xt = ctx.enter_context(nc.sbuf_tensor("xt1", [P, 2, KT, N], F32R))
        e = dict(
            raw=ctx.enter_context(nc.sbuf_tensor("experts_raw", [P, HT * TILE], F32)),
            sel=ctx.enter_context(nc.sbuf_tensor("sel", [96, NRT * P], BF16)),
            pt=ctx.enter_context(nc.sbuf_tensor("probs_t", [96, N], BF16)),
        )
        weights_in = semaphore(nc, ctx, "weights_in")
        with ExitStack() as inner:
            e["sel32"] = inner.enter_context(nc.sbuf_tensor("sel32", [96, NRT * P], F32))
            e["g_raw"] = inner.enter_context(nc.sbuf_tensor("g_raw", [P, KT * P], F32))
            e["gb"] = inner.enter_context(nc.sbuf_tensor("gb", [P, NE], F32))
            e["small"] = semaphore(nc, inner, "r_small")

            gate = inner.enter_context(nc.sbuf_tensor("gate", [P, 2, KT, P], F32R))
            logits = e["logits"] = inner.enter_context(nc.sbuf_tensor("logits", [NE, N], F32))
            log_ps = [inner.enter_context(nc.psum_tensor(f"log_ps{k}", [P, 2 * T], F32)) for k in range(2)]
            gate_ready, log_done, logits_ready = (semaphore(nc, inner, n) for n in ("gate_ready", "log_done", "logits_ready"))
            e["logits_ready"] = logits_ready
            SPLIT, BEHIND = 4, 5

            def flat(a):
                return a.rearrange("p k n -> p (k n)")

            def copy_logits(b):
                nc.scalar.wait_ge(log_done, b + 1)
                nc.scalar.copy(logits[:, b * T:(b + 1) * T], log_ps[b % 2][0:NE, 0:T]).then_inc(logits_ready, 1)

            def gate_high(s):
                if s == SPLIT:
                    nc.scalar.wait_ge(e["small"], 48)
                    nc.scalar.copy(flat(gate[:, 0, :, :]), e["g_raw"][:, :]).then_inc(gate_ready, 1)
                if s > BEHIND:
                    copy_logits(s - BEHIND - 1)

            def gate_low(s):
                if s == SPLIT:
                    nc.vector.wait_ge(gate_ready, 1)
                    nc.vector.tensor_tensor(flat(gate[:, 1, :, :]), e["g_raw"][:, :], flat(gate[:, 0, :, :]).bitcast(F32),
                                            ALU.subtract).then_inc(gate_ready, 1)

            def pair_logits(s):
                if s >= BEHIND:
                    b = s - BEHIND
                    at = slice(b * T, (b + 1) * T)
                    if b == 0:
                        nc.tensor.wait_ge(gate_ready, 2)
                    nc.tensor.wait_ge(m.low_ready, b + 1)
                    wait(nc.tensor, logits_ready, b - 1)
                    split_matmul(nc.tensor, log_ps[b % 2][:, 0:T], [(gate[:, 0, k, :], gate[:, 1, k, :]) for k in range(KT)],
                                 [(m.xt[:, 0, k, at], m.xt[:, 1, k, at]) for k in range(KT)], True, True).then_inc(log_done, 1)

            e["copy_logits"] = copy_logits

            def load(sp):
                for name, io in (("g_raw", "gate"), ("gb", "gb"), ("sel32", "sel")):
                    sp.dma_start(e[name][:, :], m.io[io]).then_inc(e["small"], 16)
                load_tiles(sp, m, e, weights_in, 0, 6)

            norm_transpose(nc, m, "n1", prefetch=load, aside=dict(act=gate_high, dve=gate_low, pe=pair_logits))
            router(nc, m, e)
        experts(nc, m, e, weights_in)


HALF = HEADS1 // 2
STACK = 3 * HD + 2


def load_stacks(sp, m, a, of, half, n, done):
    hs = slice(half * HALF, (half + 1) * HALF)
    for j, part in enumerate(((0, 1, 0), (0, 0, 1))[of]):
        sp.dma_start(a["stacks"][of][j * HD:(j + 1) * HD, hs, :].bitcast(F32),
                     m.io["qk_scratch"][of, part, half, :, ds(n * T, T)].rearrange("(h d) t -> d h t", h=HALF)
                     ).then_inc(done, 16)


def load_open(sp, m, a, half, n, done):
    sp.dma_start(a["stacks"][0][3 * HD:STACK, half * HALF:(half + 1) * HALF, :].bitcast(F32),
                 m.io["open_scratch"][ds(n * HEADS1 + half * HALF, HALF), :, :].rearrange("h k t -> k h t")).then_inc(done, 16)


def windowed_projections(nc, m, a):
    JOBS = 2 * NCH
    with ExitStack() as ctx:
        def sb(name, shape, dt=F32):
            return ctx.enter_context(nc.sbuf_tensor(name, shape, dt))

        def sem(name):
            return semaphore(nc, ctx, name)

        def bank(name):
            return ctx.enter_context(nc.psum_tensor(name, [P, 512], F32))

        qk = sb("wqk", [P, 2, 2, 2, 2, CH], F32R)
        shut = sb("wshut", [P, 2, T], F32R)
        raw, bqk, bv, ones, w_in, small = a["raw"], a["bqk"], a["bv"], a["ones"], a["w_in"], a["small"]
        wqkv = sb("wqkv", [P, 2, 3, KT, D], F32R)
        flags = sb("kflag_rounded", [2, T], F32R)
        square = sb("square", [P, 2, 2, CH])
        norms = sb("norms", [P, T + 2])
        best = sb("nbest", [P, 8])
        open_ = sb("open", [P, T])
        qk_ps = [bank(f"qk_ps{k}") for k in range(4)]
        v_ps = [bank("v_ps0"), bank("v_ps1")]
        n_ps = bank("n_ps")
        w_high, w_low = sem("wqkv_high"), sem("wqkv_low")
        qk_done, v_done, high, low, v_out, squared, norm_step = (
            sem("wqk_done"), sem("wv_done"), sem("whigh"), sem("wlow"), sem("wv_out"), sem("wsquared"), sem("wnorm_step"))
        chain, ready, open_stored, stacks_in, flags_ready = (
            sem("wchain"), sem("wready"), sem("wopen_stored"), sem("wstacks_in"), sem("wflags_ready"))
        stored = [[sem(f"wstored{of}{r}") for r in range(2)] for of in range(2)]
        block = ctx.enter_context(nc.Block())

        @block.sync
        def _(sp):
            sp.wait_ge(flags_ready, 1)
            sp.dma_start(a["stacks"][1][3 * HD:STACK, :, :].bitcast(F32),
                         flags[:, :].bitcast(F32).rearrange("k (o t) -> k o t", o=1).to_broadcast([2, HEADS1, T])
                         ).then_inc(stacks_in, 16)

            def store(of, c):
                sp.wait_ge(low, of * JOBS + 2 * c + 2)
                for part in range(2):
                    sp.dma_start(m.io["qk_scratch"][of, part, :, :, c * CH:(c + 1) * CH].rearrange("f p t -> p f t"),
                                 qk[:, of, c % 2, part, :, :].bitcast(F32)).then_inc(stored[of][c % 2], 16)

            def load(of):
                sp.wait_ge(stored[of][0], 64)
                for half in range(2):
                    load_stacks(sp, m, a, of, half, 0, stacks_in)

            for c in range(NCH):
                store(0, c)
            store(1, 0)
            load(0)
            for c in range(1, NCH):
                store(1, c)
            load(1)
            sp.wait_ge(ready, 4)
            sp.dma_start(m.io["open_scratch"], shut[:, :, :].bitcast(F32)).then_inc(open_stored, 16)
            sp.wait_ge(open_stored, 16)
            for half in range(2):
                load_open(sp, m, a, half, 0, stacks_in)
            sp.wait_ge(stacks_in, 16 * (1 + 12 + 2))
            for of in range(2):
                sp.wait_ge(stored[of][1], 64)

        @block.gpsimd
        def _(pool):
            pool.wait_ge(small, 64)
            pool.tensor_copy(flags[:, :], a["kflag"][:, :]).then_inc(flags_ready, 1)
            pool.memset(a["alone"][:, :, :, :], 0.0)

        @block.scalar
        def _(act):
            act.wait_ge(w_in, 16)
            for k in range(3):
                act.copy(wqkv[:, 0, k].rearrange("p k n -> p (k n)"), raw[:, k * KT * D:(k + 1) * KT * D]).then_inc(w_high, 1)
            act.wait_ge(small, 64)
            for i in range(2 * JOBS):
                of, c, f = i // JOBS, i % JOBS // 2, i % 2
                if c >= 2:
                    act.wait_ge(stored[of][c % 2], 32)
                act.wait_ge(qk_done, i + 1)
                act.activation(qk[:, of, c % 2, 0, f, :], qk_ps[i % 4][:, :], ACT.Identity,
                               bias=bqk[:, 2 * of + f:2 * of + f + 1]).then_inc(high, 1)
                if of == 0:
                    wait(act, norm_step, 4 * (c - 1))
                    act.activation(square[:, c % 2, f, :], qk_ps[i % 4][:, :], ACT.Square, bias=bqk[:, f:f + 1]).then_inc(squared, 1)

        @block.vector
        def _(dve):
            n = 0

            def next_(ins):
                nonlocal n
                ins.then_inc(chain, 1)
                n += 1
                dve.wait_ge(chain, n)

            def lower(i):
                of, c, f = i // JOBS, i % JOBS // 2, i % 2
                dve.wait_ge(high, i + 1)
                if of == 0:
                    dve.wait_ge(squared, i + 1)
                dve.scalar_tensor_tensor(out=qk[:, of, c % 2, 1, f, :], in0=qk_ps[i % 4][:, :],
                                         scalar=bqk[:, 2 * of + f:2 * of + f + 1],
                                         in1=qk[:, of, c % 2, 0, f, :].bitcast(F32), op0=ALU.add, op1=ALU.subtract).then_inc(low, 1)

            def search(k):
                next_(dve.max(best[:, :], norms[:, 0:T]))
                left = NGLOBAL - 8 * k
                if left < 8:
                    next_(dve.memset(best[:, left:8], -2.0))
                next_(dve.match_replace(norms[:, :], best[:, :], norms[:, :], -1.0))

            for k in range(3):
                dve.wait_ge(w_high, k + 1)
                dve.tensor_tensor(wqkv[:, 1, k].rearrange("p k n -> p (k n)"), raw[:, k * KT * D:(k + 1) * KT * D],
                                  wqkv[:, 0, k].rearrange("p k n -> p (k n)").bitcast(F32), ALU.subtract).then_inc(w_low, 1)
            dve.wait_ge(small, 64)
            next_(dve.memset(norms[:, T:T + 2], -2.0))
            for i in range(JOBS):
                lower(i)
            SEARCHES = -(-NGLOBAL // 8)
            for c in range(NCH):
                for f in range(2):
                    lower(JOBS + 2 * c + f)
                if c == 0:
                    dve.wait_ge(norm_step, 4 * NCH)
                    next_(dve.tensor_copy(norms[:, 0:T], n_ps[:, 0:T]))
                for k in range(2):
                    dve.wait_ge(v_done, 2 * c + k + 1)
                    for u in range(2):
                        t = 4 * c + 2 * k + u
                        ins = dve.tensor_tensor(a["v"][:, t * D:(t + 1) * D], v_ps[k][:, u * D:(u + 1) * D], bv[:, :], ALU.add)
                    ins.then_inc(v_out, 1)
                    if 2 * c + k >= 1:
                        search(2 * c + k - 1)
            for k in range(2 * NCH - 1, SEARCHES):
                search(k)
            next_(dve.tensor_scalar(open_[:, :], norms[:, 0:T], -1.0, -1.0e30, ALU.not_equal, ALU.mult))
            dve.memset(norms[:, 0:T], 0.0)
            next_(dve.memset(open_[:, 0:T:T - 1], 0.0))
            for k in range(2):
                own = slice(k * P, k * P + P)
                other = slice(P - k * P, 2 * P - k * P)
                dve.tensor_copy(shut[:, k, own], open_[:, own]).then_inc(ready, 1)
                dve.tensor_copy(shut[:, k, other], norms[:, other]).then_inc(ready, 1)

        @block.tensor
        def _(pe):
            def norm(c):
                pe.wait_ge(squared, 2 * c + 2)
                for s in range(2):
                    for j in range(2):
                        first = (2 * c + s) * HEADS1 + j * HALF
                        pe.matmul(n_ps[:, 0:T], ones[:, P - HALF - first:2 * P - HALF - first], square[:, c % 2, j, s * T:(s + 1) * T],
                                  start=c == 0 and s == 0 and j == 0, stop=c == NCH - 1 and s == 1 and j == 1
                                  ).then_inc(norm_step, 1)

            def project(i):
                of, c, f = i // JOBS, i % JOBS // 2, i % 2
                at = slice(c * CH, (c + 1) * CH)
                wait(pe, low, i - 3)
                ws = [tuple(wqkv[:, q, of, k, f * P:(f + 1) * P] for q in range(2)) for k in range(KT)]
                split_matmul(pe, qk_ps[i % 4][:, :], ws, [(m.xt[:, 0, k, at], m.xt[:, 1, k, at]) for k in range(KT)],
                             True, True).then_inc(qk_done, 1)

            pe.wait_ge(w_low, 1)
            pe.wait_ge(small, 64)
            for c in range(NCH):
                for f in range(2):
                    project(2 * c + f)
                if c >= 1:
                    norm(c - 1)
            pe.wait_ge(w_low, 3)
            for c in range(NCH):
                for f in range(2):
                    project(JOBS + 2 * c + f)
                if c == 0:
                    norm(NCH - 1)
                for k in range(2):
                    wait(pe, v_out, 2 * (c - 1) + k + 1)
                    for u in range(2):
                        t = 4 * c + 2 * k + u
                        xs = [tuple(m.xt[:, q, kt, t * P:(t + 1) * P] for q in range(2)) for kt in range(KT)]
                        mm = split_matmul(pe, v_ps[k][:, u * D:(u + 1) * D], xs,
                                          [(wqkv[:, 0, 2, kt, :], wqkv[:, 1, 2, kt, :]) for kt in range(KT)], True, True)
                    mm.then_inc(v_done, 1)


def windowed_heads(nc, m, a):
    PAIRS = HEADS1 // 2
    QUAD = PAIRS // 2
    SCALE = HD ** -0.5
    LS, LEXP, LT, LV, LCOPY, LTURN, LOUT = 0, 1, 2, 3, 4, 5, 6
    LBRANCH, LNORM, LSUM = 6, 7, 8
    LOADS = 7
    with ExitStack() as ctx:
        def sb(name, shape, dt=F32):
            return ctx.enter_context(nc.sbuf_tensor(name, shape, dt))

        def sem(name):
            return semaphore(nc, ctx, name)

        (qs, ks), alone = a["stacks"], a["alone"]
        probs = sb("wprobs", [P, 2, 4 * T])
        top = sb("wtop", [P, 2, 4])
        neg = sb("wneg", [P, 2, 4])
        pt = sb("wpt", [P, 2, 2, 2 * T])
        total = sb("wtotal", [P, 2, 2, HALF])
        inv = sb("winv", [P, 2, 2, HALF])
        context = sb("wcontext", [P, 2, T])
        s_ps = [ctx.enter_context(nc.psum_tensor(f"ws_ps{k}", [P, 4, T], F32)) for k in range(2)]
        t_ps = [ctx.enter_context(nc.psum_tensor(f"wt_ps{k}", [P, 2 * T], F32)) for k in range(2)]
        o_ps = [ctx.enter_context(nc.psum_tensor(f"wo_ps{k}", [P, 2, T], F32)) for k in range(2)]
        stack_in = [sem("stack_in0"), sem("stack_in1")]
        s_done, neg_ready, exp_ready, t_done, pt_ready, o_done = (
            sem("ws_done"), sem("wneg_ready"), sem("wexp_ready"), sem("wt_done"), [sem("wpt0"), sem("wpt1")], sem("wo_done"))
        top_ready, alone_ready, inv_ready, context_ready, back_done, o_out, pause = (
            sem("wtop_ready"), sem("walone_ready"), sem("winv_ready"), sem("wcontext_ready"),
            sem("wback_done"), sem("wo_out"), sem("wpause"))
        x = Residual(nc, ctx, m, "r2", 1)
        block = ctx.enter_context(nc.Block())

        def steps(eng, body):
            lagged_steps(eng, NSEQ, PAIRS, LSUM, body)

        def ends(s):
            return s and s[1] == PAIRS - 1

        def ends_half(s):
            return s and s[1] % QUAD == QUAD - 1

        @block.sync
        def _(sp):
            with sp.Fori(1, NSEQ) as n:
                for half in range(2):
                    sp.wait_ge(s_done, n * PAIRS - PAIRS + (half + 1) * QUAD)
                    for of in range(2):
                        load_stacks(sp, m, a, of, half, n, stack_in[half])
                    load_open(sp, m, a, half, n, stack_in[half])

        @block.gpsimd
        def _(pool):
            def values(n, half):
                src = a["v"][:, ds(n * 2 * D, 2 * D)].rearrange("p (k f h d) -> p k f h d", k=2, f=2, h=HALF)
                pool.tensor_copy(alone[:, half, :, :].rearrange("p k (h d) -> p k h d", h=HALF)[:, :, :, 0:HD],
                                 src[:, :, half, :, :]).then_inc(alone_ready, 1)

            x.start(pool)

            def step(at):
                if s := at(LS):
                    n, j = s
                    if j % (QUAD - 1) == 0 and j < QUAD:
                        half = j // (QUAD - 1)
                        wait(pool, o_done, (n - 1) * PAIRS + (half + 1) * QUAD if not (isinstance(n, int) and n == 0) else 0)
                        pool.sem_inc(pause, 1)
                        values(n, half)
                if ends(s := at(LBRANCH)):
                    x.factors(pool, 0, s[0], 0)
                if ends(s := at(LNORM)):
                    x.add(pool, s[0], 0)
                if ends(s := at(LSUM)):
                    x.factors(pool, 1, s[0], 0)
            steps(pool, step)

        @block.tensor
        def _(pe):
            def step(at):
                if s := at(LS):
                    n, j = s
                    g = n * PAIRS + j
                    if j % QUAD == 0:
                        wait(pe, stack_in[j // QUAD], n * (16 * LOADS))
                    wait(pe, exp_ready, g - 1)
                    for u in range(2):
                        for t in range(2):
                            mm = pe.matmul(s_ps[j % 2][:, 2 * u + t, :], qs[:, 2 * j + u, t * P:(t + 1) * P], ks[:, 2 * j + u, :],
                                           start=True, stop=True)
                    mm.then_inc(s_done, 1)
                if s := at(LT):
                    n, j = s
                    g = n * PAIRS + j
                    pe.wait_ge(exp_ready, g + 1)
                    for u in range(2):
                        wait(pe, pt_ready[u], g)
                        for t in range(2):
                            for k in range(2):
                                mm = pe.transpose(t_ps[u][:, k * T + t * P:k * T + (t + 1) * P],
                                                  probs[:, j % 2, (2 * u + t) * T + k * P:(2 * u + t) * T + (k + 1) * P], m.ident[:, :])
                        mm.then_inc(t_done, 1)
                if s := at(LV):
                    n, j = s
                    g = n * PAIRS + j
                    half = j // QUAD
                    if j % QUAD == 0:
                        pe.wait_ge(alone_ready, n * 2 + half + 1)
                        wait(pe, o_out, n * 2 + half - 1)
                    for u in range(2):
                        pe.wait_ge(pt_ready[u], g + 1)
                        h = 2 * (j % QUAD) + u
                        for k in range(2):
                            mm = pe.matmul(o_ps[half][:, 0, :], alone[:, half, k, h * P:(h + 1) * P], pt[:, j % 2, u, k * T:(k + 1) * T],
                                           start=h == 0 and k == 0, stop=h == HALF - 1 and k == 1)
                    mm.then_inc(o_done, 1)
                if ends_half(s := at(LTURN)):
                    n, j = s
                    half = j // QUAD
                    pe.wait_ge(context_ready, n * 2 + half + 1)
                    for t in range(2):
                        mm = pe.transpose(o_ps[half][:, 1, t * P:(t + 1) * P], context[:, half, t * P:(t + 1) * P], m.ident[:, :])
                    mm.then_inc(back_done, 1)
            steps(pe, step)

        @block.scalar
        def _(act):
            def step(at):
                if s := at(LEXP):
                    n, j = s
                    g = n * PAIRS + j
                    half = j // QUAD
                    act.wait_ge(neg_ready, g + 1)
                    wait(act, t_done, 2 * g - 2)
                    if j % QUAD == 0:
                        wait(act, inv_ready, n * 2 + half - 1)
                    for u in range(2):
                        for t in range(2):
                            h = 2 * (j % QUAD) + u
                            ins = act.activation(probs[:, j % 2, (2 * u + t) * T:(2 * u + t + 1) * T], s_ps[j % 2][:, 2 * u + t, :],
                                                 ACT.Exp, bias=neg[:, j % 2, 2 * u + t:2 * u + t + 1], scale=SCALE,
                                                 accum_out=total[:, half, t, h:h + 1])
                    ins.then_inc(exp_ready, 1)
                if ends_half(s := at(LCOPY)):
                    n, j = s
                    half = j // QUAD
                    act.wait_ge(o_done, n * PAIRS + j + 1)
                    act.copy(context[:, half, :], o_ps[half][:, 0, :]).then_inc(context_ready, 1)
                if s := at(LT):
                    n, j = s
                    g = n * PAIRS + j
                    act.wait_ge(t_done, 2 * g + 1)
                    wait(act, o_done, g - 1)
                    act.copy(pt[:, j % 2, 0, :], t_ps[0][:, :]).then_inc(pt_ready[0], 1)
                if ends(s := at(LNORM)):
                    x.norm(act, s[0], 0)
            steps(act, step)

        @block.vector
        def _(dve):
            def step(at):
                if s := at(LS):
                    n, j = s
                    g = n * PAIRS + j
                    dve.wait_ge(s_done, g + 1)
                    dve.tensor_reduce(top[:, j % 2, :], s_ps[j % 2][:, :, :], AX.X, ALU.max).then_inc(top_ready, 1)
                    wait(dve, exp_ready, g - 1)
                    dve.wait_ge(top_ready, g + 1)
                    dve.tensor_scalar(neg[:, j % 2, :], top[:, j % 2, :], -SCALE, None, ALU.mult).then_inc(neg_ready, 1)
                if s := at(LT):
                    n, j = s
                    g = n * PAIRS + j
                    dve.wait_ge(t_done, 2 * g + 2)
                    wait(dve, o_done, g - 1)
                    dve.tensor_copy(pt[:, j % 2, 1, :], t_ps[1][:, :]).then_inc(pt_ready[1], 1)
                if ends_half(s := at(LV)):
                    n, j = s
                    half = j // QUAD
                    dve.wait_ge(exp_ready, n * PAIRS + j + 1)
                    wait(dve, o_out, n * 2 + half - 1)
                    dve.reciprocal(inv[:, half, :, :], total[:, half, :, :]).then_inc(inv_ready, 1)
                if ends_half(s := at(LOUT)):
                    n, j = s
                    half = j // QUAD
                    dve.wait_ge(back_done, n * 2 + half + 1)
                    dve.wait_ge(inv_ready, n * 2 + half + 1)
                    dve.tensor_tensor(m.branch[:, ds(n * 2 * D, 2 * D)].rearrange("p (t f h d) -> p t f h d", t=2, f=2, h=HALF)[:, :, half],
                                      o_ps[half][:, 1, :].rearrange("p (t h d) -> p t h d", t=2, h=HALF),
                                      inv[:, half, :, :].rearrange("p t (h o) -> p t h o", o=1).to_broadcast([P, 2, HALF, HD]),
                                      ALU.mult).then_inc(o_out, 1)
                if ends(s := at(LBRANCH)):
                    x.moments_branch(dve, s[0], 0, o_out, s[0] * 2 + 2)
                if ends(s := at(LSUM)):
                    x.moments_x(dve, s[0], 0)
            steps(dve, step)


def windowed_attention(nc, m):
    with ExitStack() as ctx:
        def sb(name, shape, dt=F32, ctx=ctx):
            return ctx.enter_context(nc.sbuf_tensor(name, shape, dt))

        a = dict(
            v=sb("wv", [P, NT * D]),
            stacks=(sb("q_stack", [STACK, HEADS1, T], F32R), sb("k_stack", [STACK, HEADS1, T], F32R)),
            alone=sb("values_alone", [P, 2, 2, HALF * (P + HD)]),
        )
        with ExitStack() as inner:
            m.xt = sb("xt2", [P, 2, KT, N], F32R, inner)
            a["raw"] = sb("qkv_raw", [P, 3 * KT * D], F32, inner)
            a["bqk"] = sb("bqk", [P, 4], F32, inner)
            a["bv"] = sb("bv", [P, D], F32, inner)
            a["ones"] = sb("ones_block", [P, HALF + 2 * (P - HALF)], F32, inner)
            a["kflag"] = sb("kflag", [2, T], F32, inner)
            a["w_in"], a["small"] = semaphore(nc, inner, "wqkv_in"), semaphore(nc, inner, "wsmall")

            def load(sp):
                sp.dma_start(a["raw"][:, :], m.io["wqkv"]).then_inc(a["w_in"], 16)
                for name in ("bqk", "bv", "ones", "kflag"):
                    sp.dma_start(a[name][:, :], m.io[name]).then_inc(a["small"], 16)

            transpose_norm(nc, m, "n2", load)
            windowed_projections(nc, m, a)
        windowed_heads(nc, m, a)


def quantised_feed_forward(nc, m):
    ZERO = 128.0
    LUP, LHID, LDOWN, LOUT = 0, 1, 2, 3
    LBRANCH, LNORM = (4, 5), (5, 6)
    UP = KT * HIDT * P
    with ExitStack() as ctx:
        def sb(name, shape, dt=F32):
            return ctx.enter_context(nc.sbuf_tensor(name, shape, dt))

        def sem(name):
            return semaphore(nc, ctx, name)

        def bank(name):
            return ctx.enter_context(nc.psum_tensor(name, [P, 512], F32))

        m.xt = sb("xt3", [P, 2, KT, N], F32R)
        CODES = 2 * UP + HIDT * D
        codes = sb("codes", [P, CODES], I32)
        wts = sb("qweights", [P, CODES], F32R)
        scales = sb("qscales", [P, 2 * HIDT])
        s_down = sb("s_down", [P, D])
        small, codes_in = sem("qsmall"), sem("codes_in")
        def load(sp):
            sp.dma_start(codes[:, :], m.io["codes"]).then_inc(codes_in, 16)
            sp.dma_start(scales[:, :], m.io["scales"]).then_inc(small, 16)
            sp.dma_start(s_down[:, :], m.io["s_down"]).then_inc(small, 16)

        HALFWAY = CODES // 2

        def low_codes(s):
            if s == NSEQ + 1:
                nc.vector.wait_ge(codes_in, 16)
                nc.vector.tensor_scalar(wts[:, :HALFWAY], codes[:, :HALFWAY], ZERO, None, ALU.subtract)

        def high_codes(s):
            if s == NSEQ + 1:
                nc.scalar.wait_ge(codes_in, 16)
                nc.scalar.activation(wts[:, HALFWAY:], codes[:, HALFWAY:], ACT.Copy, bias=-ZERO)

        transpose_norm(nc, m, "n3", load, aside=dict(dve=low_codes, act=high_codes))
        gated = sb("qgated", [P, 2, CH])
        hid = sb("qhid", [P, 2, CH])
        h = sb("qh", [P, 2, 2, CH], F32R)
        gate_ps, up_ps, o_ps = [[bank(f"{n}{k}") for k in range(2)] for n in ("qg_ps", "qu_ps", "qo_ps")]
        up_done, gated_ready, hid_ready, h_high, h_low, down_done, o_out = (
            sem("qup_done"), sem("qgated_ready"), sem("qhid_ready"), sem("qh_high"), sem("qh_low"), sem("qdown_done"), sem("qo_out"))
        x = Residual(nc, ctx, m, "r3", 2)
        stored = sem("out_stored")
        block = ctx.enter_context(nc.Block())

        def ends(s):
            return s and s[1] == HIDT - 1

        def steps(eng, body):
            lagged_steps(eng, NCH, HIDT, LNORM[1], body)

        @block.sync
        def _(sp):
            with sp.Fori(0, NSEQ) as b:
                sp.wait_ge(x.x_final, x.final(b))
                sp.dma_start(m.io["out"][ds(b * T, T), :].rearrange("(u p) d -> p u d", p=P),
                             m.x[:, ds(b * 2 * D, 2 * D)].rearrange("p (u d) -> p u d", u=2)
                             ).then_inc(stored, 16)
            sp.wait_ge(stored, 16 * NSEQ)

        @block.gpsimd
        def _(pool):
            x.start(pool)

            def step(at):
                for u in range(2):
                    if ends(s := at(LBRANCH[u])):
                        x.factors(pool, 0, s[0] * 2 + u, u)
                for u in range(2):
                    if ends(s := at(LNORM[u])):
                        x.add(pool, s[0] * 2 + u, u)
            steps(pool, step)

        @block.scalar
        def _(act):
            act.wait_ge(small, 32)

            def step(at):
                if s := at(LUP):
                    c, k = s
                    g = c * HIDT + k
                    act.wait_ge(up_done, g + 1)
                    wait(act, hid_ready, g - 1)
                    act.activation(gated[:, k % 2, :], gate_ps[k % 2][:, :], ACT.Silu, scale=scales[:, k:k + 1]).then_inc(gated_ready, 1)
                if s := at(LHID):
                    c, k = s
                    g = c * HIDT + k
                    act.wait_ge(hid_ready, g + 1)
                    wait(act, down_done, g - 1)
                    act.copy(h[:, k % 2, 0, :], hid[:, k % 2, :]).then_inc(h_high, 1)
                for u in range(2):
                    if ends(s := at(LNORM[u])):
                        x.norm(act, s[0] * 2 + u, u)
            steps(act, step)

        @block.vector
        def _(dve):
            dve.wait_ge(small, 32)

            def step(at):
                if s := at(LUP):
                    c, k = s
                    g = c * HIDT + k
                    dve.wait_ge(gated_ready, g + 1)
                    wait(dve, h_low, g - 1)
                    dve.scalar_tensor_tensor(out=hid[:, k % 2, :], in0=up_ps[k % 2][:, :], scalar=scales[:, HIDT + k:HIDT + k + 1],
                                             in1=gated[:, k % 2, :], op0=ALU.mult, op1=ALU.mult).then_inc(hid_ready, 1)
                if s := at(LHID):
                    c, k = s
                    g = c * HIDT + k
                    dve.wait_ge(h_high, g + 1)
                    dve.tensor_tensor(h[:, k % 2, 1, :], hid[:, k % 2, :], h[:, k % 2, 0, :].bitcast(F32), ALU.subtract).then_inc(h_low, 1)
                if s := at(LDOWN):
                    c, k = s
                    if k == HIDT - 1:
                        dve.wait_ge(down_done, (c + 1) * HIDT)
                        for t in range(2):
                            ins = dve.tensor_tensor(m.branch[:, ds(c * 4 * D + t * 2 * D, 2 * D)].rearrange("p (u d) -> p u d", u=2),
                                                    o_ps[t][:, :].rearrange("p (u d) -> p u d", u=2),
                                                    s_down[:, :].rearrange("p (u d) -> p u d", u=1).to_broadcast([P, 2, D]), ALU.mult)
                        ins.then_inc(o_out, 1)
                for u in range(2):
                    if ends(s := at(LBRANCH[u])):
                        x.moments_branch(dve, s[0] * 2 + u, u, o_out, s[0] + 1)
            steps(dve, step)

        @block.tensor
        def _(pe):
            def step(at):
                if s := at(LUP):
                    c, k = s
                    g = c * HIDT + k
                    wait(pe, hid_ready, g - 1)
                    for o, base in ((gate_ps, 0), (up_ps, UP)):
                        for kt in range(KT):
                            for part in range(2):
                                mm = pe.matmul(o[k % 2][:, :], wts[:, base + (kt * HIDT + k) * P:base + (kt * HIDT + k + 1) * P],
                                               m.xt[:, part, kt, ds(c * CH, CH)], start=kt == 0 and part == 0,
                                               stop=kt == KT - 1 and part == 1)
                    mm.then_inc(up_done, 1)
                if s := at(LDOWN):
                    c, k = s
                    g = c * HIDT + k
                    if k == 0:
                        wait(pe, o_out, c)
                    pe.wait_ge(h_low, g + 1)
                    for t in range(4):
                        for part in range(2):
                            mm = pe.matmul(o_ps[t // 2][:, (t % 2) * D:(t % 2 + 1) * D], h[:, k % 2, part, t * P:(t + 1) * P],
                                           wts[:, 2 * UP + k * D:2 * UP + (k + 1) * D], start=k == 0 and part == 0 and t % 2 == 0,
                                           stop=k == HIDT - 1 and part == 1, skip_group_check=True)
                    mm.then_inc(down_done, 1)
            steps(pe, step)


def program(nc, io):
    with ExitStack() as ctx:
        m = Memory(nc, ctx, io)
        with ExitStack() as inner:
            m.xt = inner.enter_context(nc.sbuf_tensor("xt0", [P, 2, KT, N], F32R))
            latent_attention(nc, m)
        mixture(nc, m)
        windowed_attention(nc, m)
        quantised_feed_forward(nc, m)


def scratch(nc):
    return {
        "qk_scratch": nc.dram_tensor("qk_scratch", (2, 2, 2, P, N), F32, kind="Internal").ap(),
        "open_scratch": nc.dram_tensor("open_scratch", (P, 2, T), F32, kind="Internal").ap(),
    }


def layout(x):
    import numpy as np
    f = {k: np.asarray(v) for k, v in x.items()}
    turn = np.concatenate([np.arange(0, LAT, 2), np.arange(1, LAT, 2)])

    def rows(w):
        return np.ascontiguousarray(w.reshape(-1, P, w.shape[-1]).transpose(1, 0, 2).reshape(P, -1))

    def wide(v):
        return np.ascontiguousarray(np.broadcast_to(v, (P, v.shape[0])))

    ang = np.arange(T, dtype=np.float32)[:, None] * (
        np.float32(10000.0) ** (-np.arange(LAT // 2, dtype=np.float32) / np.float32(LAT // 2)))[None, :]
    cos, sin = np.cos(ang).T, np.sin(ang).T
    causal = np.where(np.arange(P)[:, None] >= np.arange(P)[None, :], np.float32(0), np.float32(LOWEST))
    heads = np.arange(HEADS0) * LAT
    pad = NSH * P - HE
    wide1, wide3 = (np.concatenate([f[f"L0_ffn_{w}_shared"], np.zeros((D, pad), np.float32),
                                    f[f"L0_ffn_{w}_routed"].transpose(1, 0, 2).reshape(D, NE * HE)], axis=1)
                    for w in ("w1", "w3"))
    tall2 = np.concatenate([f["L0_ffn_w2_shared"], np.zeros((pad, D), np.float32),
                            f["L0_ffn_w2_routed"].reshape(NE * HE, D)])
    ups = [w.reshape(KT, P, HT, P).transpose(1, 2, 0, 3).reshape(P, HT, KT * P) for w in (wide1, wide3)]
    tiles = np.concatenate([*ups, tall2.reshape(HT, P, D).transpose(1, 0, 2)], axis=2)
    ones = np.zeros((P, HALF + 2 * (P - HALF)), np.float32)
    ones[np.arange(P), P - HALF + np.arange(P) // HD] = 1
    kflag = np.stack([np.arange(T) >= P + P // 2, np.arange(T) < P // 2]).astype(np.float32)
    hpad = HIDT * P - HID
    codes = [np.pad(f["L1_ffn_wq_gate"].T, ((0, 0), (0, hpad)), constant_values=128),
             np.pad(f["L1_ffn_wq_up"].T, ((0, 0), (0, hpad)), constant_values=128),
             np.pad(f["L1_ffn_wq_down"].T, ((0, hpad), (0, 0)), constant_values=128)]
    scales = [np.pad(f[f"L1_ffn_s_{w}"], (0, hpad)) for w in ("gate", "up")]
    gate = np.zeros((D, P), np.float32)
    gate[:, :NE] = f["L0_ffn_gate_w"].T
    sel = (np.arange(96)[:, None] % 32 == np.arange(NRT * P)[None, :] // HE)
    io = {
        "x": f["L0_attn_x"].reshape(N, D),
        "ident": np.eye(P, dtype=np.float32),
        "wl": rows(f["L0_attn_W_latent"][:, turn]),
        "bl": f["L0_attn_b_latent"][turn].reshape(P, 1),
        "wd": rows(f["L0_attn_W_d"][:, (heads[:, None] + turn[None]).ravel()]),
        "bd": np.ascontiguousarray(f["L0_attn_b_d"].reshape(HEADS0, LAT)[:, turn].T),
        "wp": rows(f["L0_attn_W_proj"][(heads[:, None] + turn[None]).ravel(), :]),
        "bproj": wide(f["L0_attn_b_proj"]),
        "trig": np.stack([np.concatenate([cos, cos]), np.concatenate([sin, -sin])], axis=1).astype(np.float32),
        "experts": tiles.reshape(P, HT * TILE),
        "gate": rows(gate), "gb": wide(f["L0_ffn_gate_b"]),
        "sel": sel.astype(np.float32),
        "wqkv": np.concatenate([rows(f[f"L1_attn_W{w}"]) for w in "qkv"], axis=1),
        "bqk": np.concatenate([f["L1_attn_bq"].reshape(2, P), f["L1_attn_bk"].reshape(2, P)]).T,
        "bv": wide(f["L1_attn_bv"]),
        "ones": ones, "kflag": kflag,
        "codes": np.concatenate([*(rows(c) for c in codes)], axis=1),
        "scales": np.concatenate([s.reshape(HIDT, P) for s in scales]).T,
        "s_down": wide(f["L1_ffn_s_down"]),
        "mask": np.concatenate([causal, np.zeros((P, P), np.float32), causal], axis=1),
    }
    return {k: np.ascontiguousarray(v) for k, v in io.items()}


def kernel(**inputs):
    import numpy as np
    from concourse import bacc
    from concourse.bass_utils import run_bass_kernel_spmd

    nc = bacc.Bacc("TRN2", target_bir_lowering=False, num_devices=1)
    arrays = layout(inputs)
    io = {k: nc.dram_tensor(f"in_{k}", a.shape, mybir.dt.from_np(a.dtype), kind="ExternalInput").ap()
          for k, a in arrays.items()}
    io |= scratch(nc)
    io["out"] = nc.dram_tensor("out_x", (N, D), F32, kind="ExternalOutput").ap()
    program(nc, io)
    r = run_bass_kernel_spmd(nc, [{f"in_{k}": a for k, a in arrays.items()}], core_ids=[0])
    return np.asarray(r.results[0]["out_x"]).reshape(NSEQ, T, D)
```
